# Optimizing a Trainium2 kernel written in Bass

```python
import numpy as np
import jax
import jax.numpy as jnp

def _softmax(x, axis=-1):
    return jax.nn.softmax(x, axis=axis)

def _gelu(x):
    return jax.nn.gelu(x, approximate=True)

def _silu(x):
    return jax.nn.silu(x)

def _sigmoid(x):
    return jax.nn.sigmoid(x)

def _layernorm(x, axis=-1, eps=1e-05):
    m = jnp.mean(x, axis=axis, keepdims=True)
    v = jnp.var(x, axis=axis, keepdims=True)
    return (x - m) / jnp.sqrt(v + eps)

def _scatter_add(tgt, idx, src, axis=0):
    return tgt.at[idx].add(src)

def _segment_sum(src, seg, n):
    return jax.ops.segment_sum(src, seg, n)
kernel_name = 'mk_adaln_attn_ffn_d1_seqx_r8_ff1708'

def setup_inputs(seed: int=0):
    np.random.seed(seed)
    _w = jnp.asarray

    def _rec_inputs():
        import jax
        import jax.numpy as jnp
        _rk = jax.random.key(seed)
        x = -7.109e-05 + 0.9999 * jax.random.normal(jax.random.fold_in(_rk, 1), (32, 128, 128), jnp.float32)
        _lenS = 128 - jax.random.randint(jax.random.fold_in(_rk, 7), (32,), 0, max(1, 128 // 4) + 1, jnp.int32)
        _lenS2 = 128 - jax.random.randint(jax.random.fold_in(_rk, 8), (32,), 0, max(1, 128 // 4) + 1, jnp.int32)
        itok_B_0_8 = jax.random.randint(jax.random.fold_in(_rk, 11), (32,), 0, 9, jnp.int32)
        fside_Bx8_0 = jax.random.uniform(jax.random.fold_in(_rk, 12), (32, 8), jnp.float32, 0.0, 0.556406)
        condB_sharedgateprob = jax.random.uniform(jax.random.fold_in(_rk, 13), (32,), jnp.float32, 0.0, 0.794948)
        return (x, itok_B_0_8, fside_Bx8_0, condB_sharedgateprob)
    x, itok_B_0_8, fside_Bx8_0, condB_sharedgateprob = _rec_inputs()

    def _L0_cond_setup():
        import jax, jax.numpy as jnp
        import numpy as np
        LN_EPS = 1e-05
        key = jax.random.key(seed)
        ks = jax.random.split(key, 8)
        B, S, H, A, L = (32, 256, 128, 32, 10)
        return {'hidden_states': jax.random.normal(ks[0], (B, S, H), dtype=jnp.float32), 'language_ids': jax.random.randint(ks[1], (B,), 0, L, dtype=jnp.int64), 'W1': jax.random.normal(ks[2], (L, H, A), dtype=jnp.float32) * (1.0 / np.sqrt(H)), 'b1': jnp.zeros((L, A), dtype=jnp.float32), 'W2': jax.random.normal(ks[3], (L, A, H), dtype=jnp.float32) * (1.0 / np.sqrt(A)), 'b2': jnp.zeros((L, H), dtype=jnp.float32), 'gamma': jnp.ones((L, H), dtype=jnp.float32), 'beta': jnp.zeros((L, H), dtype=jnp.float32)}
    _L0_cond_all = _L0_cond_setup()
    _L0_cond_in = {k: v for k, v in _L0_cond_all.items() if k in ('W1', 'b1', 'W2', 'b2', 'gamma', 'beta')}
    del _L0_cond_all

    def _L0_attn_setup():
        import jax, jax.numpy as jnp
        import numpy as np
        D_MODEL = 128
        NUM_LAYERS = 4
        D_STATE = 16
        D_CONV = 4
        EXPAND = 2
        D_INNER = EXPAND * D_MODEL
        DT_RANK = (D_MODEL + 15) // 16
        B, L = (4, 256)
        EPS = 1e-05

        def layer_norm(x, w, b):
            mu = jnp.mean(x, axis=-1, keepdims=True)
            var = jnp.mean(jnp.square(x - mu), axis=-1, keepdims=True)
            return (x - mu) * jax.lax.rsqrt(var + EPS) * w + b

        def mamba_block(x, Wi, cw, cb, Wx, Wdt, bdt, Alog, Dp, Wo):
            b, l, _ = x.shape
            xz = x @ Wi.T
            xs, z = jnp.split(xz, 2, axis=-1)
            xc = jnp.swapaxes(xs, 1, 2)
            xc = jax.lax.conv_general_dilated(xc, cw[:, None, :], (1,), [(D_CONV - 1, 0)], feature_group_count=D_INNER, dimension_numbers=('NCW', 'OIW', 'NCW'))
            u = jax.nn.silu(jnp.swapaxes(xc, 1, 2) + cb)
            xdbl = u @ Wx.T
            dt, Bc, Cc = jnp.split(xdbl, [DT_RANK, DT_RANK + D_STATE], axis=-1)
            dt = jax.nn.softplus(dt @ Wdt.T + bdt)
            A = -jnp.exp(Alog)

            def step(h, inp):
                dt_t, B_t, C_t, u_t = inp
                dA = jnp.exp(dt_t[:, :, None] * A)
                h = dA * h + dt_t[:, :, None] * B_t[:, None, :] * u_t[:, :, None]
                y = jnp.einsum('bds,bs->bd', h, C_t)
                return (h, y)
            h0 = jnp.zeros((b, D_INNER, D_STATE), x.dtype)
            xs_t = (jnp.swapaxes(dt, 0, 1), jnp.swapaxes(Bc, 0, 1), jnp.swapaxes(Cc, 0, 1), jnp.swapaxes(u, 0, 1))
            _, ys = jax.lax.scan(step, h0, xs_t)
            y = jnp.swapaxes(ys, 0, 1) + u * Dp
            y = y * jax.nn.silu(z)
            return y @ Wo.T
        key = jax.random.key(seed)
        ks = jax.random.split(key, 12)
        s = 0.02
        nl = NUM_LAYERS
        inp = {'x': jax.random.normal(ks[0], (B, L, D_MODEL), jnp.float32), 'W_in': jax.random.normal(ks[1], (nl, 2 * D_INNER, D_MODEL), jnp.float32) * s, 'conv_w': jax.random.normal(ks[2], (nl, D_INNER, D_CONV), jnp.float32) * s, 'conv_b': jnp.zeros((nl, D_INNER), jnp.float32), 'W_x': jax.random.normal(ks[3], (nl, DT_RANK + 2 * D_STATE, D_INNER), jnp.float32) * s, 'W_dt': jax.random.normal(ks[4], (nl, D_INNER, DT_RANK), jnp.float32) * s, 'b_dt': jnp.full((nl, D_INNER), -4.6, jnp.float32), 'A_log': jnp.broadcast_to(jnp.log(jnp.arange(1, D_STATE + 1, dtype=jnp.float32)), (nl, D_INNER, D_STATE)) * jnp.ones((nl, D_INNER, 1), jnp.float32), 'Dp': jnp.ones((nl, D_INNER), jnp.float32), 'W_out': jax.random.normal(ks[5], (nl, D_MODEL, D_INNER), jnp.float32) * s, 'ln_w': jnp.ones((nl, D_MODEL), jnp.float32), 'ln_b': jnp.zeros((nl, D_MODEL), jnp.float32)}
        return inp
    _L0_attn_all = _L0_attn_setup()
    _L0_attn_in = {k: v for k, v in _L0_attn_all.items() if k in ('W_in', 'conv_w', 'conv_b', 'W_x', 'W_dt', 'b_dt', 'A_log', 'Dp', 'W_out', 'ln_w', 'ln_b')}
    del _L0_attn_all

    def _L0_cond2_setup():
        import jax, jax.numpy as jnp
        import numpy as np
        E, B, S, D, F = (8, 2, 128, 128, 512)
        key = jax.random.key(seed)
        ks = jax.random.split(key, 9)
        sc_d = 1.0 / np.sqrt(D)
        sc_f = 1.0 / np.sqrt(F)
        hidden_states = jax.random.normal(ks[0], (B, S, D), dtype=jnp.float32)
        gating_probs = jax.nn.softmax(jax.random.normal(ks[1], (B, E), dtype=jnp.float32), axis=-1)
        shared_gate_prob = jax.nn.sigmoid(jax.random.normal(ks[2], (B, 1), dtype=jnp.float32))
        Wg = jax.random.normal(ks[3], (E, D, F), dtype=jnp.float32) * sc_d
        Wu = jax.random.normal(ks[4], (E, D, F), dtype=jnp.float32) * sc_d
        Wd = jax.random.normal(ks[5], (E, F, D), dtype=jnp.float32) * sc_f
        Sg = jax.random.normal(ks[6], (D, F), dtype=jnp.float32) * sc_d
        Su = jax.random.normal(ks[7], (D, F), dtype=jnp.float32) * sc_d
        Sd = jax.random.normal(ks[8], (F, D), dtype=jnp.float32) * sc_f
        return {'hidden_states': hidden_states, 'gating_probs': gating_probs, 'shared_gate_prob': shared_gate_prob, 'Wg': Wg, 'Wu': Wu, 'Wd': Wd, 'Sg': Sg, 'Su': Su, 'Sd': Sd}
    _L0_cond2_all = _L0_cond2_setup()
    _L0_cond2_in = {k: v for k, v in _L0_cond2_all.items() if k in ('Wg', 'Wu', 'Wd', 'Sg', 'Su', 'Sd')}
    del _L0_cond2_all

    def _L0_ffn_setup():
        import jax, jax.numpy as jnp
        import numpy as np
        B, S, D, E, F = (4, 256, 128, 8, 512)
        key = jax.random.key(seed)
        k0, k1, k2, k3 = jax.random.split(key, 4)
        x = jax.random.normal(k0, (B, S, D), dtype=jnp.float32)
        wg = jax.random.normal(k1, (D, E), dtype=jnp.float32) * 0.02
        w_gate = jax.random.normal(k2, (E, D, F), dtype=jnp.float32) * 0.02
        w_down = jax.random.normal(k3, (E, F, D), dtype=jnp.float32) * 0.02
        return {'x': x, 'wg': wg, 'w_gate': w_gate, 'w_down': w_down}
    _L0_ffn_all = _L0_ffn_setup()
    _L0_ffn_in = {k: v for k, v in _L0_ffn_all.items() if k in ('wg', 'w_gate', 'w_down')}
    del _L0_ffn_all
    return {'x': x, 'itok_B_0_8': itok_B_0_8, 'fside_Bx8_0': fside_Bx8_0, 'condB_sharedgateprob': condB_sharedgateprob, 'L0_cond_W1': _L0_cond_in['W1'], 'L0_cond_b1': _L0_cond_in['b1'], 'L0_cond_W2': _L0_cond_in['W2'], 'L0_cond_b2': _L0_cond_in['b2'], 'L0_cond_gamma': _L0_cond_in['gamma'], 'L0_cond_beta': _L0_cond_in['beta'], 'L0_attn_W_in': _L0_attn_in['W_in'], 'L0_attn_conv_w': _L0_attn_in['conv_w'], 'L0_attn_conv_b': _L0_attn_in['conv_b'], 'L0_attn_W_x': _L0_attn_in['W_x'], 'L0_attn_W_dt': _L0_attn_in['W_dt'], 'L0_attn_b_dt': _L0_attn_in['b_dt'], 'L0_attn_A_log': _L0_attn_in['A_log'], 'L0_attn_Dp': _L0_attn_in['Dp'], 'L0_attn_W_out': _L0_attn_in['W_out'], 'L0_attn_ln_w': _L0_attn_in['ln_w'], 'L0_attn_ln_b': _L0_attn_in['ln_b'], 'L0_cond2_Wg': _L0_cond2_in['Wg'], 'L0_cond2_Wu': _L0_cond2_in['Wu'], 'L0_cond2_Wd': _L0_cond2_in['Wd'], 'L0_cond2_Sg': _L0_cond2_in['Sg'], 'L0_cond2_Su': _L0_cond2_in['Su'], 'L0_cond2_Sd': _L0_cond2_in['Sd'], 'L0_ffn_wg': _L0_ffn_in['wg'], 'L0_ffn_w_gate': _L0_ffn_in['w_gate'], 'L0_ffn_w_down': _L0_ffn_in['w_down']}

def reference(x, itok_B_0_8, fside_Bx8_0, condB_sharedgateprob, L0_cond_W1, L0_cond_b1, L0_cond_W2, L0_cond_b2, L0_cond_gamma, L0_cond_beta, L0_attn_W_in, L0_attn_conv_w, L0_attn_conv_b, L0_attn_W_x, L0_attn_W_dt, L0_attn_b_dt, L0_attn_A_log, L0_attn_Dp, L0_attn_W_out, L0_attn_ln_w, L0_attn_ln_b, L0_cond2_Wg, L0_cond2_Wu, L0_cond2_Wd, L0_cond2_Sg, L0_cond2_Su, L0_cond2_Sd, L0_ffn_wg, L0_ffn_w_gate, L0_ffn_w_down):
    import jax
    import jax.numpy as jnp

    def _L0_cond_ref(hidden_states, language_ids, W1, b1, W2, b2, gamma, beta):
        import jax, jax.numpy as jnp
        import numpy as np
        LN_EPS = 1e-05
        w1 = W1[language_ids]
        w2 = W2[language_ids]
        h = jnp.einsum('bsh,bha->bsa', hidden_states, w1) + b1[language_ids][:, None, :]
        h = jax.nn.relu(h)
        adapted = jnp.einsum('bsa,bah->bsh', h, w2) + b2[language_ids][:, None, :]
        x = hidden_states + adapted
        mean = jnp.mean(x, axis=-1, keepdims=True)
        var = jnp.mean(jnp.square(x - mean), axis=-1, keepdims=True)
        normed = (x - mean) * jax.lax.rsqrt(var + LN_EPS)
        return normed * gamma[language_ids][:, None, :] + beta[language_ids][:, None, :]

    def _L0_attn_ref(x, W_in, conv_w, conv_b, W_x, W_dt, b_dt, A_log, Dp, W_out, ln_w, ln_b):
        import jax, jax.numpy as jnp
        import numpy as np
        D_MODEL = 128
        NUM_LAYERS = 4
        D_STATE = 16
        D_CONV = 4
        EXPAND = 2
        D_INNER = EXPAND * D_MODEL
        DT_RANK = (D_MODEL + 15) // 16
        B, L = (4, 256)
        EPS = 1e-05

        def layer_norm(x, w, b):
            mu = jnp.mean(x, axis=-1, keepdims=True)
            var = jnp.mean(jnp.square(x - mu), axis=-1, keepdims=True)
            return (x - mu) * jax.lax.rsqrt(var + EPS) * w + b

        def mamba_block(x, Wi, cw, cb, Wx, Wdt, bdt, Alog, Dp, Wo):
            b, l, _ = x.shape
            xz = x @ Wi.T
            xs, z = jnp.split(xz, 2, axis=-1)
            xc = jnp.swapaxes(xs, 1, 2)
            xc = jax.lax.conv_general_dilated(xc, cw[:, None, :], (1,), [(D_CONV - 1, 0)], feature_group_count=D_INNER, dimension_numbers=('NCW', 'OIW', 'NCW'))
            u = jax.nn.silu(jnp.swapaxes(xc, 1, 2) + cb)
            xdbl = u @ Wx.T
            dt, Bc, Cc = jnp.split(xdbl, [DT_RANK, DT_RANK + D_STATE], axis=-1)
            dt = jax.nn.softplus(dt @ Wdt.T + bdt)
            A = -jnp.exp(Alog)

            def step(h, inp):
                dt_t, B_t, C_t, u_t = inp
                dA = jnp.exp(dt_t[:, :, None] * A)
                h = dA * h + dt_t[:, :, None] * B_t[:, None, :] * u_t[:, :, None]
                y = jnp.einsum('bds,bs->bd', h, C_t)
                return (h, y)
            h0 = jnp.zeros((b, D_INNER, D_STATE), x.dtype)
            xs_t = (jnp.swapaxes(dt, 0, 1), jnp.swapaxes(Bc, 0, 1), jnp.swapaxes(Cc, 0, 1), jnp.swapaxes(u, 0, 1))
            _, ys = jax.lax.scan(step, h0, xs_t)
            y = jnp.swapaxes(ys, 0, 1) + u * Dp
            y = y * jax.nn.silu(z)
            return y @ Wo.T
        for i in range(NUM_LAYERS):
            x = mamba_block(layer_norm(x, ln_w[i], ln_b[i]), W_in[i], conv_w[i], conv_b[i], W_x[i], W_dt[i], b_dt[i], A_log[i], Dp[i], W_out[i]) + x
        return x

    def _L0_cond2_ref(hidden_states, gating_probs, shared_gate_prob, Wg, Wu, Wd, Sg, Su, Sd):
        import jax, jax.numpy as jnp
        import numpy as np
        E, B, S, D, F = (8, 2, 128, 128, 512)
        h = hidden_states
        g = jnp.einsum('bsd,edf->ebsf', h, Wg)
        u = jnp.einsum('bsd,edf->ebsf', h, Wu)
        expert_outs = jnp.einsum('ebsf,efd->ebsd', jax.nn.silu(g) * u, Wd)
        expert_output = jnp.einsum('be,ebsd->bsd', gating_probs, expert_outs)
        shared = jnp.einsum('bsf,fd->bsd', jax.nn.silu(h @ Sg) * (h @ Su), Sd)
        sg = shared_gate_prob[:, :, None]
        return (1.0 - sg) * expert_output + sg * shared

    def _L0_ffn_ref(x, wg, w_gate, w_down):
        import jax, jax.numpy as jnp
        import numpy as np
        B, S, D, E, F = (4, 256, 128, 8, 512)
        Bb, Ss, Dd = x.shape
        Ee = wg.shape[1]
        T = Bb * Ss
        C = 2 * T // Ee
        tokens = x.reshape(T, Dd)
        logits = tokens.astype(jnp.float32) @ wg.astype(jnp.float32)
        gates = jax.nn.softmax(logits, axis=-1)
        idx1 = jnp.argmax(gates, axis=-1)
        mask1 = jax.nn.one_hot(idx1, Ee, dtype=jnp.int32)
        logits_no1 = jnp.where(mask1 > 0, -jnp.inf, logits)
        idx2 = jnp.argmax(logits_no1, axis=-1)
        mask2 = jax.nn.one_hot(idx2, Ee, dtype=jnp.int32)
        g1 = jnp.take_along_axis(gates, idx1[:, None], axis=-1)[:, 0]
        g2 = jnp.take_along_axis(gates, idx2[:, None], axis=-1)[:, 0]
        denom = jnp.clip(g1 + g2, 1e-09, None)
        g1, g2 = (g1 / denom, g2 / denom)
        loc1 = jnp.cumsum(mask1, axis=0) - mask1
        loc2 = jnp.cumsum(mask2, axis=0) - mask2 + jnp.sum(mask1, axis=0, keepdims=True)
        loc1_s = jnp.sum(loc1 * mask1, axis=-1)
        loc2_s = jnp.sum(loc2 * mask2, axis=-1)
        keep1 = (loc1_s < C).astype(x.dtype)
        keep2 = (loc2_s < C).astype(x.dtype)
        f1 = idx1 * C + jnp.minimum(loc1_s, C - 1)
        f2 = idx2 * C + jnp.minimum(loc2_s, C - 1)
        disp = jnp.zeros((Ee * C, Dd), dtype=x.dtype)
        disp = disp.at[f1].add(tokens * keep1[:, None])
        disp = disp.at[f2].add(tokens * keep2[:, None])
        disp = disp.reshape(Ee, C, Dd)
        h = jax.nn.gelu(jnp.einsum('ecd,edf->ecf', disp, w_gate), approximate=False)
        eo = jnp.einsum('ecf,efd->ecd', h, w_down).reshape(Ee * C, Dd)
        out = (g1 * keep1)[:, None].astype(x.dtype) * eo[f1] + (g2 * keep2)[:, None].astype(x.dtype) * eo[f2]
        return out.reshape(Bb, Ss, Dd)
    x = x + _L0_attn_ref(_L0_cond_ref(x, itok_B_0_8, L0_cond_W1, L0_cond_b1, L0_cond_W2, L0_cond_b2, L0_cond_gamma, L0_cond_beta), L0_attn_W_in, L0_attn_conv_w, L0_attn_conv_b, L0_attn_W_x, L0_attn_W_dt, L0_attn_b_dt, L0_attn_A_log, L0_attn_Dp, L0_attn_W_out, L0_attn_ln_w, L0_attn_ln_b)
    x = x + _L0_ffn_ref(_L0_cond2_ref(x, fside_Bx8_0, condB_sharedgateprob[:, None], L0_cond2_Wg, L0_cond2_Wu, L0_cond2_Wd, L0_cond2_Sg, L0_cond2_Su, L0_cond2_Sd), L0_ffn_wg, L0_ffn_w_gate, L0_ffn_w_down)
    return x

_drawn_inputs = setup_inputs


def setup_inputs(seed=0):
    import zlib

    import numpy as np

    out = dict(_drawn_inputs(seed))
    spreads = {'L0_cond_b1': (0.0, 0.1),
     'L0_cond_b2': (0.0, 0.1),
     'L0_cond_gamma': (1.0, 0.2),
     'L0_cond_beta': (0.0, 0.1),
     'L0_attn_conv_b': (0.0, 0.8),
     'L0_attn_b_dt': (-4.599999904632568, 0.6),
     'L0_attn_Dp': (1.0, 0.6),
     'L0_attn_ln_w': (1.0, 0.6),
     'L0_attn_ln_b': (0.0, 0.8)}
    factors = {'L0_attn_W_in': 8.0,
     'L0_attn_conv_w': 8.0,
     'L0_attn_W_x': 8.0,
     'L0_attn_W_dt': 8.0,
     'L0_attn_A_log': 8.0,
     'L0_attn_W_out': 8.0}
    for name, (base, spread) in spreads.items():
        noise = np.random.default_rng([zlib.crc32(name.encode()), seed]).standard_normal(out[name].shape)
        drawn = base * np.exp(spread * noise) if base else spread * noise
        out[name] = jnp.asarray(drawn.astype(out[name].dtype))
    for name, factor in factors.items():
        out[name] = (out[name] * factor).astype(out[name].dtype)
    return out
```

```python
import concourse.bass as bass
from concourse import mybir
from contextlib import ExitStack

NSEQ, T, D = 32, 128, 128
NL, DI, NS, NTAP = 4, 256, 16, 4
DTR = 8
NX = 2 * NS + DTR
G = 4
NG = NSEQ // G
TOK = G * T
NH = DI // 128
NIT = NL * NG
ADP, NLANG = 32, 10
NE, F, NF = 8, 512, 4
NE1 = NE + 1
CAP = 2 * NSEQ * T // NE
NSLOT = NE * CAP
NCH = CAP // 128
EPS = 1e-5
CR = 8
NDA, NDB, NHB, NGB, NCS = 2, 2, 2, 4, 2
RLAG = 3
WUSE = 9
LNEXP = "natural_log_exp_and_others"
FAR = 65536.0

f32, bf16, i32, u32 = mybir.dt.float32, mybir.dt.bfloat16, mybir.dt.int32, mybir.dt.uint32
ALU, ACT, AX = mybir.AluOpType, mybir.ActivationFunctionType, mybir.AxisListType
ds = bass.ds


def setup_phase(nc, A, K, M):
    ctx = ExitStack()
    with ctx:
        def sb(name, shape, dt=f32):
            return ctx.enter_context(nc.sbuf_tensor(name, shape, dt))

        def sem(name):
            return ctx.enter_context(nc.semaphore(name))

        ids = sb("ids", [1, NSEQ], i32)
        xg = [sb(f"xg{p}", [128, G, D]) for p in range(2)]
        w1 = [sb(f"ad_w1{p}", [128, G, ADP]) for p in range(2)]
        w2 = [sb(f"ad_w2{p}", [64, G, D]) for p in range(2)]
        b1 = [sb(f"ad_b1{p}", [ADP, G]) for p in range(2)]
        gb = [sb(f"ad_gb{p}", [128, G, 2, D]) for p in range(2)]
        xT = sb("ad_xT", [128, TOK])
        hT = sb("ad_hT", [64, TOK])
        y = sb("ad_y", [128, G, D])
        nrm = sb("ad_nrm", [128, G, D])
        stats = sb("ad_stats", [128, G, 6])
        mv = sb("ad_mv", [128, G, 2])
        vare = sb("ad_vare", [128, G])
        rstd = sb("ad_rstd", [128, G])
        spare = sb("ad_spare", [128, 1])
        wraw = sb("wraw", [128, NL, DI])
        cwb = sb("cwb", [128, NL * NTAP * DI])
        psT = ctx.enter_context(nc.psum_tensor("ad_psT", [128, 512], f32))
        psH = ctx.enter_context(nc.psum_tensor("ad_psH", [128, 512], f32))
        psA = ctx.enter_context(nc.psum_tensor("ad_psA", [128, 512], f32))

        ids_ld, raw_ld, w_ld, moe_ld, ad_ld = sem("ids_ld"), sem("raw_ld"), sem("w_ld"), sem("moe_ld"), [sem("ad_ld0"), sem("ad_ld1")]
        cst, tapped, xTd, xTc, hTd, hTc, summed = (sem(n) for n in ("cst", "tapped", "xTd", "xTc", "hTd", "hTc", "summed"))
        ysum, stat, var_ok, rstd_ok, normed, placed, pch, a_ok = (
            sem(n) for n in ("ysum", "stat", "var_ok", "rstd_ok", "normed", "placed", "pch", "a_ok"))
        NAD = 1 + 6 * G

        with nc.Block() as block:
            @block.sync
            def _(sp):
                sp.dma_start(ids[:, :], A["ids"]).then_inc(ids_ld, 16)
                sp.wait_ge(ids_ld, 16)
                sp.sem_inc(placed, CR)

                def load(j, p):
                    g = 2 * j + p
                    sp.wait_ge(placed, CR + g - 1)
                    sp.dma_start(xg[p][:, :, :], A["x"][ds(g * G, G), :, :].rearrange("b t d -> t b d")).then_inc(ad_ld[p], 16)
                    for q in range(G):
                        lid = sp.value_load(ids[0:1, ds(g * G + q, 1)], min_val=0, max_val=NLANG - 1)
                        one = ds(lid, 1)
                        sp.dma_start(w1[p][:, q, :], A["W1"][one, :, :].rearrange("o h a -> (o h) a")).then_inc(ad_ld[p], 16)
                        sp.dma_start(w2[p][0:ADP, q, :], A["W2"][one, :, :].rearrange("o h a -> (o h) a")).then_inc(ad_ld[p], 16)
                        sp.dma_start(w2[p][ADP:ADP + 1, q, :], A["b2"][one, :]).then_inc(ad_ld[p], 16)
                        sp.dma_start(b1[p][:, q:q + 1], A["b1"][one, :].rearrange("o a -> a o")).then_inc(ad_ld[p], 16)
                        for c, n in enumerate(("gamma", "beta")):
                            sp.dma_start(gb[p][:, q, c, :], A[n][one, :].broadcast_to([128, D])).then_inc(ad_ld[p], 16)

                with sp.Fori(0, NG // 2) as j:
                    load(j, 0)
                    load(j, 1)

            @block.scalar
            def _(act):
                act.dma_start(wraw[:, :, :], A["W_inT"][:, :, 0:DI].rearrange("l m d -> m l d")).then_inc(raw_ld, 16)
                act.dma_start(cwb[:, :], A["conv_wT"].rearrange("l k d -> (l k d)").unsqueeze(0).broadcast_to([128, NL * NTAP * DI])).then_inc(raw_ld, 16)
                act.dma_start(M["negA"][:, :, :], A["A_log"]).then_inc(w_ld, 16)
                act.dma_start(M["wz"][:, :, :], A["W_inT"][:, :, DI:2 * DI].rearrange("l m d -> m l d")).then_inc(w_ld, 16)
                act.dma_start(M["wx"][:, :, :], A["W_xT"].rearrange("l (c p) r -> p (l c) r", p=128)).then_inc(w_ld, 16)
                act.dma_start(M["wdt"][32:32 + DTR, :, :], A["W_dtT"].rearrange("l r d -> r l d")).then_inc(w_ld, 16)
                act.dma_start(M["wo"][:, :, :], A["W_outT"].rearrange("l (c p) m -> p (l c) m", p=128)).then_inc(w_ld, 16)
                act.dma_start(M["par"][:, :, :], A["par"]).then_inc(w_ld, 16)
                act.dma_start(K["wgu"][:, 0:NE, 0, :], A["Wg"].rearrange("e d f -> d e f")).then_inc(moe_ld, 16)
                act.dma_start(K["wgu"][:, 0:NE, 1, :], A["Wu"].rearrange("e d f -> d e f")).then_inc(moe_ld, 16)
                act.dma_start(K["wgu"][:, NE, 0, :], A["Sg"]).then_inc(moe_ld, 16)
                act.dma_start(K["wgu"][:, NE, 1, :], A["Su"]).then_inc(moe_ld, 16)
                act.dma_start(K["wbc"][:, 0:NE, :], A["gateT"].rearrange("e b -> (e b)").unsqueeze(0).broadcast_to([128, NE * NSEQ]).rearrange("p (e b) -> p e b", e=NE)).then_inc(moe_ld, 16)
                act.dma_start(K["sgp"][:, :], A["sgate"].broadcast_to([128, NSEQ])).then_inc(moe_ld, 16)
                act.dma_start(K["wr"][:, :], A["wg"]).then_inc(moe_ld, 16)
                act.sem_inc(xTc, CR)
                act.sem_inc(hTc, CR)
                act.wait_ge(w_ld, 16 * 6)
                act.activation(M["negA"][:, :, :], M["negA"][:, :, :], ACT.Exp).then_inc(a_ok, 1)

                def adapter(j, p):
                    g = 2 * j + p
                    act.wait_ge(xTd, CR + g + 1)
                    act.wait_ge(hTd, CR + g)
                    act.activation(xT[:, :], psT[:, :], ACT.Copy).then_inc(xTc, 1)
                    act.wait_ge(hTd, CR + g + 1)
                    act.wait_ge(summed, CR + g)
                    for q in range(G):
                        ins = act.activation(hT[0:ADP, q * T:(q + 1) * T], psH[0:ADP, q * T:(q + 1) * T], ACT.Relu, bias=b1[p][:, q:q + 1])
                    ins.then_inc(hTc, 1)

                with act.Fori(0, NG // 2) as j:
                    adapter(j, 0)
                    adapter(j, 1)
                act.wait_ge(moe_ld, 16 * 7)

            @block.gpsimd
            def _(pool):
                n = 0

                def link(ins):
                    nonlocal n
                    n += 1
                    ins.then_inc(pch, 1)
                    pool.wait_ge(pch, n)

                pool.sem_inc(rstd_ok, CR)
                link(pool.memset(K["ident"][:, :], 0.0))
                link(pool.affine_select(out=K["ident"][:, :], in_=K["ident"][:, :], compare_op=ALU.not_equal, fill=1.0,
                                        base=0, pattern=[[-1, 128]], channel_multiplier=1))
                link(pool.memset(K["eps"][:, :], EPS))
                link(pool.memset(K["nhalf"][:, :], -0.5))
                link(pool.memset(hT[32:33, :], 1.0))
                pool.memset(M["zpad"], 0.0).then_inc(cst, 1)
                link(pool.memset(M["sel"][:, :, :], 0.0))
                for q in range(3):
                    link(pool.affine_select(out=M["sel"][:, :, :], in_=M["sel"][:, :, :], compare_op=ALU.not_equal, fill=1.0,
                                            base=-32 * q, pattern=[[-1, 2 * NS], [0, 128]], channel_multiplier=1))
                with pool.Fori(0, NG) as g:
                    pool.wait_ge(stat, CR + g + 1)
                    pool.tensor_tensor(vare[:, :], mv[:, :, 1], K["eps"][:, :], ALU.add).then_inc(var_ok, 1)
                    pool.wait_ge(var_ok, g + 1)
                    pool.tensor_tensor(rstd[:, :], vare[:, :], K["nhalf"][:, :], ALU.pow).then_inc(rstd_ok, 1)
                pool.wait_ge(raw_ld, 32)
                for l in range(NL):
                    for k in range(NTAP):
                        pool.tensor_tensor(M["taps"][:, l, k, :], wraw[:, l, :], cwb[:, (l * NTAP + k) * DI:(l * NTAP + k + 1) * DI], ALU.mult)

            @block.tensor
            def _(pe):
                pe.sem_inc(xTd, CR)
                pe.sem_inc(hTd, CR)
                pe.sem_inc(summed, CR)
                pe.wait_ge(cst, 1)

                def adapter(j, p):
                    g = 2 * j + p
                    pe.wait_ge(ad_ld[p], 16 * NAD * (j + 1))
                    pe.wait_ge(xTc, CR + g)
                    for q in range(G):
                        ins = pe.transpose(psT[:, q * T:(q + 1) * T], xg[p][:, q, :], K["ident"][:, :])
                    ins.then_inc(xTd, 1)
                    pe.wait_ge(xTc, CR + g + 1)
                    pe.wait_ge(hTc, CR + g)
                    for q in range(G):
                        ins = pe.matmul(psH[0:ADP, q * T:(q + 1) * T], lhsT=w1[p][:, q, :], rhs=xT[:, q * T:(q + 1) * T], start=True, stop=True)
                    ins.then_inc(hTd, 1)
                    pe.wait_ge(hTc, CR + g + 1)
                    pe.wait_ge(ysum, CR + g)
                    for q in range(G):
                        ins = pe.matmul(psA[:, q * T:(q + 1) * T], lhsT=hT[0:ADP + 1, q * T:(q + 1) * T], rhs=w2[p][0:ADP + 1, q, :], start=True, stop=True)
                    ins.then_inc(summed, 1)

                with pe.Fori(0, NG // 2) as j:
                    adapter(j, 0)
                    adapter(j, 1)

            @block.vector
            def _(dve):
                dve.sem_inc(ysum, CR)
                dve.sem_inc(stat, CR)
                dve.sem_inc(normed, CR)
                dve.wait_ge(a_ok, 1)
                dve.tensor_scalar(M["negA"][:, :, :], M["negA"][:, :, :], -1.0, None, ALU.mult)
                dve.wait_ge(moe_ld, 16 * 7)
                dve.tensor_scalar(K["wbc"][:, NE, :], K["sgp"][:, :], -1.0, 1.0, ALU.mult, ALU.add).then_inc(a_ok, 1)
                dve.wait_ge(a_ok, 2)
                dve.tensor_tensor(K["wbc"][:, 0:NE, :], K["wbc"][:, 0:NE, :], K["wbc"][:, NE, :].unsqueeze(1).broadcast_to([128, NE, NSEQ]), ALU.mult).then_inc(a_ok, 1)
                dve.wait_ge(a_ok, 3)
                dve.tensor_copy(K["wbc"][:, NE, :], K["sgp"][:, :])

                def adapter(j, p):
                    g = 2 * j + p
                    dve.wait_ge(summed, CR + g + 1)
                    dve.tensor_tensor(y[:, :, :], xg[p][:, :, :], psA[:, :].rearrange("p (q d) -> p q d", q=G), ALU.add).then_inc(ysum, 1)
                    dve.wait_ge(ysum, CR + g + 1)
                    for q in range(G):
                        ins = dve.bn_stats(stats[:, q, :], y[:, q, :])
                    ins.then_inc(normed, 1)
                    dve.wait_ge(normed, CR + 2 * g + 1)
                    dve.memset(spare[:, :], 0.0)
                    for q in range(G):
                        ins = dve.bn_aggr(mv[:, q, :], stats[:, q, :])
                    ins.then_inc(stat, 1)
                    dve.wait_ge(stat, CR + g + 1)
                    for q in range(G):
                        ins = dve.scalar_tensor_tensor(out=nrm[:, q, :], in0=y[:, q, :], scalar=mv[:, q, 0:1], in1=gb[p][:, q, 0, :], op0=ALU.subtract, op1=ALU.mult)
                    ins.then_inc(normed, 1)
                    dve.wait_ge(normed, CR + 2 * g + 2)
                    dve.wait_ge(rstd_ok, CR + g + 1)
                    for q in range(G):
                        ins = dve.scalar_tensor_tensor(out=K["h_res"][:, ds(g * G + q, 1), :].rearrange("p o d -> p (o d)"), in0=nrm[:, q, :], scalar=rstd[:, q:q + 1], in1=gb[p][:, q, 1, :], op0=ALU.mult, op1=ALU.add)
                    ins.then_inc(placed, 1)

                with dve.Fori(0, NG // 2) as j:
                    adapter(j, 0)
                    adapter(j, 1)


def mamba_phase(nc, A, K, M):
    ctx = ExitStack()
    with ctx:
        def sb(name, shape, dt=f32):
            return ctx.enter_context(nc.sbuf_tensor(name, shape, dt))

        def sem(name):
            return ctx.enter_context(nc.semaphore(name))

        taps, wz, wx, wdt, wo, par, negA, sel, xnT = (M[n] for n in ("taps", "wz", "wx", "wdt", "wo", "par", "negA", "sel", "xnT"))
        h_res, ident = K["h_res"], K["ident"]
        wcur = sb("wcur", [128, NTAP + 1, DI])
        wxcur = sb("wxcur", [128, NH, NX])
        wdcur = sb("wdcur", [64, DI])
        parc = sb("parc", [128, 8])
        Acur = [sb(f"Acur{p}", [128, NH * NS]) for p in range(2)]
        stats = sb("stats", [128, G, 6])
        mv = sb("mv", [128, G, 2])
        vare = sb("vare", [128, G])
        rstd = sb("rstd", [128, G])
        spare = sb("spare", [128, 1])
        xc = sb("xc", [128, G, D])
        u = sb("u", [128, NH, TOK])
        sz = [sb(f"sz{p}", [128, NH, TOK]) for p in range(2)]
        dt = [sb(f"dt{p}", [128, NH, G, T]) for p in range(2)]
        dtu = [sb(f"dtu{p}", [128, NH, TOK]) for p in range(2)]
        ud = sb("ud", [128, NH, TOK])
        bc3 = [sb(f"bc3{p}", [96, TOK], bf16) for p in range(2)]
        xd = sb("xd", [64, TOK])
        mid = sb("mid", [32, TOK], bf16)
        r1 = sb("r1", [32, TOK])
        vv = sb("vv", [128, NH * TOK])
        lv = sb("lv", [128, NH * TOK])
        yg = sb("yg", [128, NH, TOK])
        crs = [sb(f"crs{b}", [128, TOK]) for b in range(NCS)]
        dA = [sb(f"dA{b}", [128, NH, G, T]) for b in range(NDA)]
        dB = [sb(f"dB{b}", [128, NH, TOK]) for b in range(NDB)]
        hh = [sb(f"hh{b}", [128, NH, TOK]) for b in range(NHB)]
        gg = [sb(f"gg{b}", [128, NH, TOK]) for b in range(NGB)]
        bank = [ctx.enter_context(nc.psum_tensor(f"bank{b}", [128, 512], f32)) for b in range(8)]
        psB, psC, psW = bank[0:2], bank[2], bank[3]
        psY = [bank[4:6], bank[6:8]]

        (wcur_ld, wready, wfree, brep, crep, dbu, da, scan, ccp, prod, red, stat, moments, var_ok, rstd_ok, centred, skipped,
         par_ok, hi_ok, mid_ok, mids_ok, r1_ok, lo_ok, exp_ok, abs_ok, ln_ok, dt_ok, dtu_ok, ud_ok, ygated, zeroed) = (
            sem("m_" + n) for n in ("wcur_ld wready wfree brep crep dbu da scan ccp prod red stat moments var_ok rstd_ok centred skipped "
                                    "par_ok hi_ok mid_ok mids_ok r1_ok lo_ok exp_ok abs_ok ln_ok dt_ok dtu_ok ud_ok ygated zeroed").split())

        def loop(eng, body, first, last):
            first()
            body(0, 0, False, True)
            with eng.Fori(0, (NIT - 2) // 2) as j:
                body(2 * j + 1, 1, True, True)
                body(2 * j + 2, 0, True, True)
            body(NIT - 1, 1, True, False)
            last()

        def use(b, c):
            if isinstance(b, int) and b == NIT - 1:
                c = max(c - (WUSE - 1), 0)
            if isinstance(b, int) and b <= 0:
                return CR + (WUSE - 1) * (b + 1) + c
            return CR + WUSE * b + (WUSE - 2) + c

        use_last = use(NIT - 1, 0) - CR + 1

        def at_least(eng, sm, v):
            if not (isinstance(v, int) and v <= CR):
                eng.wait_ge(sm, v)

        with nc.Block() as block:
            @block.sync
            def _(sp):
                def weights(i):
                    lay = ds(i // NG, 1)
                    sp.dma_start(wcur[:, 0:NTAP, :], taps[:, lay, :, :].rearrange("p o k d -> p (o k) d")).then_inc(wcur_ld, 16)
                    sp.dma_start(wcur[:, NTAP:NTAP + 1, :], wz[:, lay, :]).then_inc(wcur_ld, 16)
                    sp.dma_start(wxcur[:, :, :], wx[:, ds(i // NG * NH, NH), :]).then_inc(wcur_ld, 16)
                    sp.dma_start(wdcur[32:32 + DTR, :], wdt[32:32 + DTR, lay, :].rearrange("p o d -> p (o d)")).then_inc(wcur_ld, 16)

                weights(0)
                for i in (1, 2):
                    sp.wait_ge(wready, use(i - 2, WUSE - 1))
                    weights(i)
                with sp.Fori(3, NIT) as i:
                    sp.wait_ge(wready, use(i - 2, WUSE - 1))
                    weights(i)

            @block.tensor
            def _(pe):
                for sm in (wready, brep, crep, red, skipped):
                    pe.sem_inc(sm, CR)

                def work(b, c):
                    at_least(pe, wfree, use(b, c))

                def broadcast_B(n, p, k):
                    at_least(pe, dbu, CR + n - 1)
                    pe.matmul(psB[k % 2][:, :], lhsT=sel[:, k, :], rhs=bc3[p][:, :], start=True, stop=True).then_inc(brep, 1)

                def broadcast_C(n, p, k):
                    at_least(pe, ccp, CR + n)
                    pe.matmul(psC[:, :], lhsT=sel[:, NS + k, :], rhs=bc3[p][:, :], start=True, stop=True).then_inc(crep, 1)

                def sum_states(n, p, k):
                    pe.wait_ge(prod, CR + n + 1)
                    for c in range(NH):
                        ins = pe.matmul(psY[p][c][:, :], lhsT=ident[:, :], rhs=gg[k % NGB][:, c, :], start=False, stop=(k == NS - 1))
                    ins.then_inc(red, 1)

                def skip(i, p):
                    pe.wait_ge(ud_ok, CR + i + 1)
                    at_least(pe, ygated, CR + i - 1)
                    for c in range(NH):
                        ins = pe.matmul(psY[p][c][:, :], lhsT=ident[:, :], rhs=ud[:, c, :], start=True, stop=False)
                    ins.then_inc(skipped, 1)

                def out_projection(b):
                    pe.wait_ge(ygated, CR + b)
                    work(b, 8)
                    for q in range(G):
                        for c in range(NH):
                            ins = pe.matmul(psW[:, q * T:(q + 1) * T], lhsT=yg[:, c, q * T:(q + 1) * T],
                                            rhs=wo[:, ds((b - 1) // NG * NH + c, 1), :].rearrange("p o m -> p (o m)"), start=(c == 0), stop=(c == NH - 1))
                    ins.then_inc(wready, 1)

                def pre(b, what):
                    if what == "transpose":
                        pe.wait_ge(centred, CR + b + 2)
                        work(b, 0)
                        for q in range(G):
                            ins = pe.transpose(psW[:, q * T:(q + 1) * T], xc[:, q, :], ident[:, :])
                        ins.then_inc(wready, 1)
                    if what in ("x0", "x1"):
                        c = int(what[1])
                        if c == 0:
                            pe.wait_ge(wcur_ld, 64 * (b + 2))
                        work(b, 1 + c)
                        for k in range(NTAP):
                            ins = pe.matmul(psW[:, :], lhsT=wcur[:, k, c * 128:(c + 1) * 128], rhs=xnT[:, :, k:k + T], start=(k == 0), stop=(k == NTAP - 1))
                        ins.then_inc(wready, 1)
                    if what in ("z0", "z1"):
                        c = int(what[1])
                        work(b, 3 + c)
                        pe.matmul(psW[:, :], lhsT=wcur[:, NTAP, c * 128:(c + 1) * 128], rhs=xnT[:, :, NTAP - 1:NTAP - 1 + T], start=True, stop=True).then_inc(wready, 1)
                    if what == "bcdt":
                        work(b, 5)
                        for c in range(NH):
                            ins = pe.matmul(psW[0:NX, :], lhsT=wxcur[:, c, :], rhs=u[:, c, :], start=(c == 0), stop=(c == NH - 1))
                        ins.then_inc(wready, 1)
                    if what in ("dt0", "dt1"):
                        c = int(what[2])
                        work(b, 6 + c)
                        pe.matmul(psW[:, :], lhsT=wdcur[32:32 + DTR, c * 128:(c + 1) * 128], rhs=xd[32:32 + DTR, :], start=True, stop=True).then_inc(wready, 1)

                WHAT = {3: ["transpose"], 6: ["x0"], 7: ["x1", "z0", "z1"], 8: ["bcdt"], 9: ["dt0"], 10: ["dt1"]}

                def parts(b):
                    pe.wait_ge(lo_ok, CR + b + 2)
                    pe.wait_ge(mids_ok, CR + b + 2)

                def first():
                    for k in sorted(WHAT):
                        for what in WHAT[k]:
                            pre(-1, what)
                    skip(0, 0)
                    parts(-1)
                    broadcast_B(0, 0, 0)
                    broadcast_C(0, 0, 0)

                def body(i, p, prev, more):
                    for k in range(NS):
                        n = NS * i + k
                        if k < NS - 1:
                            broadcast_B(n + 1, p, k + 1)
                            broadcast_C(n + 1, p, k + 1)
                        elif more:
                            parts(i)
                            broadcast_B(n + 1, 1 - p, 0)
                            broadcast_C(n + 1, 1 - p, 0)
                        if k >= RLAG:
                            sum_states(n - RLAG, p, k - RLAG)
                        elif prev:
                            sum_states(n - RLAG, 1 - p, NS + k - RLAG)
                        if more:
                            for what in WHAT.get(k, ()):
                                pre(i, what)
                        if prev and k == 12:
                            out_projection(i)
                        if more and k == 14:
                            skip(i + 1, 1 - p)

                def last():
                    for k in range(NS - RLAG, NS):
                        sum_states(NS * (NIT - 1) + k, 1, k)
                    pe.wait_ge(ygated, CR + NIT)
                    pe.wait_ge(wfree, CR + use_last)
                    for q in range(G):
                        for c in range(NH):
                            ins = pe.matmul(psW[:, q * T:(q + 1) * T], lhsT=yg[:, c, q * T:(q + 1) * T], rhs=wo[:, (NL - 1) * NH + c, :], start=(c == 0), stop=(c == NH - 1))
                    ins.then_inc(wready, 1)

                loop(pe, body, first, last)

            @block.scalar
            def _(act):
                for sm in (par_ok, hi_ok, mid_ok, mids_ok, exp_ok, ln_ok, da, ccp, wfree):
                    act.sem_inc(sm, CR)

                def pre(b, what, p):
                    if what == "params":
                        lay = ds((b + 1) // NG, 1)
                        at_least(act, ud_ok, CR + b + 1)
                        act.activation(parc[:, :], par[:, lay, :].rearrange("p o v -> p (o v)"), ACT.Copy)
                        act.activation(Acur[p][:, :], negA[:, lay, :].rearrange("p o v -> p (o v)"), ACT.Copy).then_inc(par_ok, 1)
                        act.wait_ge(par_ok, CR + b + 2)
                    if what == "norm":
                        act.wait_ge(wready, use(b, 1))
                        act.activation(xnT[:, :, NTAP - 1:NTAP - 1 + T], psW[:, :].rearrange("p (q t) -> p q t", q=G), ACT.Identity,
                                       scale=parc[:, 0:1], bias=parc[:, 1:2]).then_inc(wfree, 1)
                    if what in ("x0", "x1"):
                        c = int(what[1])
                        act.wait_ge(wready, use(b, 2 + c))
                        at_least(act, dtu_ok, CR + b + 1)
                        act.activation(u[:, c, :], psW[:, :], ACT.Silu, bias=parc[:, 2 + c:3 + c]).then_inc(wfree, 1)
                    if what in ("z0", "z1"):
                        c = int(what[1])
                        act.wait_ge(wready, use(b, 4 + c))
                        at_least(act, ygated, CR + b)
                        act.activation(sz[p][:, c, :], psW[:, :], ACT.Silu).then_inc(wfree, 1)
                    if what == "bcdt":
                        act.wait_ge(wready, use(b, 6))
                        at_least(act, r1_ok, CR + b + 1)
                        act.activation(xd[0:NX, :], psW[0:NX, :], ACT.Copy).then_inc(wfree, 1)
                        act.wait_ge(wfree, use(b, 6))
                        act.activation(bc3[p][0:32, :], xd[0:32, :], ACT.Copy).then_inc(hi_ok, 1)
                    if what in ("dt0", "dt1"):
                        c = int(what[2])
                        act.wait_ge(wready, use(b, 7 + c))
                        at_least(act, dt_ok, CR + b + 1)
                        act.activation(vv[:, c * TOK:(c + 1) * TOK], psW[:, :], ACT.Identity, bias=parc[:, 4 + c:5 + c]).then_inc(wfree, 1)
                    if what == "mid":
                        act.wait_ge(r1_ok, CR + b + 2)
                        at_least(act, lo_ok, CR + b + 1)
                        act.activation(mid[:, :], r1[:, :], ACT.Copy).then_inc(mid_ok, 1)
                        act.wait_ge(mid_ok, CR + b + 2)
                        act.activation(bc3[p][32:64, :], mid[:, :], ACT.Copy).then_inc(mids_ok, 1)
                    if what == "softplus":
                        act.wait_ge(abs_ok, CR + b + 2)
                        act.activation(lv[:, :], lv[:, :], ACT.Exp).then_inc(exp_ok, 1)
                        act.wait_ge(exp_ok, CR + b + 2)
                        act.activation(lv[:, :], lv[:, :], ACT.Ln, bias=1.0).then_inc(ln_ok, 1)

                WHAT = {0: ["params"], 4: ["norm"], 7: ["x0", "x1", "z0", "z1", "tables"], 8: ["bcdt"], 9: ["dt0"], 10: ["dt1", "mid"],
                        11: ["softplus"]}

                def pres(b, p, k):
                    for what in WHAT.get(k, ()):
                        if what == "tables":
                            act.preload_act_table_set(LNEXP)
                        else:
                            pre(b, what, p)

                def step(i, p, k):
                    n = NS * i + k
                    at_least(act, scan, CR + n + 1 - NDA)
                    for c in range(NH):
                        ins = act.activation(dA[k % NDA][:, c, :, 1:T], dt[p][:, c, :, 1:T], ACT.Exp, scale=Acur[p][:, c * NS + k:c * NS + k + 1])
                    ins.then_inc(da, 1)
                    act.wait_ge(crep, CR + n + 1)
                    at_least(act, prod, CR + n + 1 - NCS)
                    act.activation(crs[k % NCS][:, :], psC[:, :], ACT.Copy).then_inc(ccp, 1)

                def first():
                    for k in range(NS):
                        pres(-1, 0, k)

                def body(i, p, prev, more):
                    act.wait_ge(dt_ok, CR + i + 1)
                    for k in range(NS):
                        step(i, p, k)
                        if more:
                            pres(i, 1 - p, k)

                loop(act, body, first, lambda: None)

            @block.vector
            def _(dve):
                for sm in (lo_ok, dbu, scan, stat, moments, centred, abs_ok, dt_ok, dtu_ok, ygated):
                    dve.sem_inc(sm, CR)
                for b in range(NDA):
                    ins = dve.memset(dA[b][:, :, :, 0:1], 0.0)
                ins.then_inc(zeroed, 1)
                dve.wait_ge(zeroed, 1)

                def input_term(n, p, k):
                    dve.wait_ge(brep, CR + n + 1)
                    at_least(dve, scan, CR + n + 1 - NDB)
                    dve.tensor_tensor(dB[k % NDB][:, :, :], dtu[p][:, :, :], psB[k % 2][:, :].unsqueeze(1).broadcast_to([128, NH, TOK]), ALU.mult).then_inc(dbu, 1)

                def scan_step(n, p, k):
                    dve.wait_ge(da, CR + n + 1)
                    dve.wait_ge(dbu, CR + n + 1)
                    at_least(dve, prod, CR + n + 1 - NHB)
                    dve.tensor_tensor_scan(out=hh[k % NHB][:, :, :].rearrange("p c t -> p (c t)"), data0=dA[k % NDA][:, :, :, :].rearrange("p c q t -> p (c q t)"),
                                           data1=dB[k % NDB][:, :, :].rearrange("p c t -> p (c t)"), initial=0.0, op0=ALU.mult, op1=ALU.add).then_inc(scan, 1)

                def pre(b, what, p):
                    g = (b + 1) % NG
                    if what == "moments":
                        at_least(dve, wfree, use(b, 0))
                        for q in range(G):
                            ins = dve.bn_stats(stats[:, q, :], h_res[:, ds(g * G + q, 1), :].rearrange("p o d -> p (o d)"))
                        ins.then_inc(stat, 1)
                        dve.wait_ge(stat, CR + b + 2)
                        dve.memset(spare[:, :], 0.0)
                        for q in range(G):
                            ins = dve.bn_aggr(mv[:, q, :], stats[:, q, :])
                        ins.then_inc(moments, 1)
                    if what == "centre":
                        dve.wait_ge(rstd_ok, CR + b + 2)
                        for q in range(G):
                            ins = dve.tensor_scalar(xc[:, q, :], h_res[:, ds(g * G + q, 1), :].rearrange("p o d -> p (o d)"), mv[:, q, 0:1], rstd[:, q:q + 1], ALU.subtract, ALU.mult)
                        ins.then_inc(centred, 1)
                    if what == "lo":
                        dve.wait_ge(mid_ok, CR + b + 2)
                        dve.tensor_tensor(bc3[p][64:96, :], r1[:, :], mid[:, :], ALU.subtract).then_inc(lo_ok, 1)
                    if what == "abs":
                        dve.wait_ge(wfree, use(b, 8))
                        dve.scalar_tensor_tensor(out=lv[:, :], in0=vv[:, :], scalar=-1.0, in1=vv[:, :], op0=ALU.mult, op1=ALU.min).then_inc(abs_ok, 1)
                    if what == "dt":
                        dve.wait_ge(ln_ok, CR + b + 2)
                        at_least(dve, da, CR + NS * b)
                        dve.scalar_tensor_tensor(out=dt[p][:, :, :, :].rearrange("p c q t -> p (c q t)"), in0=vv[:, :], scalar=0.0, in1=lv[:, :], op0=ALU.max, op1=ALU.add).then_inc(dt_ok, 1)
                        dve.wait_ge(dt_ok, CR + b + 2)
                        dve.tensor_tensor(dtu[p][:, :, :].rearrange("p c t -> p (c t)"), dt[p][:, :, :, :].rearrange("p c q t -> p (c q t)"), u[:, :, :].rearrange("p c t -> p (c t)"), ALU.mult).then_inc(dtu_ok, 1)

                def gate(i, p):
                    dve.wait_ge(red, CR + NS * (i + 1))
                    at_least(dve, wready, use(i, 9))
                    for c in range(NH):
                        ins = dve.tensor_tensor(yg[:, c, :], sz[p][:, c, :], psY[p][c][:, :], ALU.mult)
                    ins.then_inc(ygated, 1)

                def residual(b):
                    dve.wait_ge(wready, use(b, 9))
                    at = ds((b - 1) % NG * G, G)
                    dve.tensor_tensor(h_res[:, at, :], h_res[:, at, :], psW[:, :].rearrange("p (q d) -> p q d", q=G), ALU.add).then_inc(wfree, 1)

                def first():
                    for what in ("moments", "centre", "abs", "lo", "dt"):
                        pre(-1, what, 0)
                    dve.wait_ge(dtu_ok, CR + 1)
                    input_term(0, 0, 0)

                def body(i, p, prev, more):
                    for k in range(NS):
                        n = NS * i + k
                        if k < NS - 1:
                            input_term(n + 1, p, k + 1)
                        elif more:
                            dve.wait_ge(dtu_ok, CR + i + 2)
                            input_term(n + 1, 1 - p, 0)
                        scan_step(n, p, k)
                        if more and k == 0:
                            pre(i, "moments", 1 - p)
                        if more and k == 2:
                            pre(i, "centre", 1 - p)
                        if prev and k == 4:
                            gate(i - 1, 1 - p)
                        if more and k == 10:
                            pre(i, "abs", 1 - p)
                        if more and k == 11:
                            pre(i, "lo", 1 - p)
                        if more and k == 12:
                            pre(i, "dt", 1 - p)
                        if prev and k == 14:
                            residual(i)

                def last():
                    gate(NIT - 1, 1)
                    dve.wait_ge(wready, CR + use_last + 1)
                    at = slice((NG - 1) * G, NG * G)
                    dve.tensor_tensor(h_res[:, at, :], h_res[:, at, :], psW[:, :].rearrange("p (q d) -> p q d", q=G), ALU.add)

                loop(dve, body, first, last)

            @block.gpsimd
            def _(pool):
                for sm in (prod, rstd_ok, r1_ok, ud_ok):
                    pool.sem_inc(sm, CR)

                def pre(b, what, p):
                    if what == "rstd":
                        pool.wait_ge(moments, CR + b + 2)
                        pool.tensor_tensor(vare[:, :], mv[:, :, 1], K["eps"][:, :], ALU.add).then_inc(var_ok, 1)
                        pool.wait_ge(var_ok, b + 2)
                        at_least(pool, centred, CR + b + 1)
                        pool.tensor_tensor(rstd[:, :], vare[:, :], K["nhalf"][:, :], ALU.pow).then_inc(rstd_ok, 1)
                    if what == "r1":
                        at_least(pool, skipped, CR + b + 1)
                        at_least(pool, lo_ok, CR + b + 1)
                        pool.wait_ge(hi_ok, CR + b + 2)
                        pool.tensor_tensor(r1[:, :], xd[0:32, :], bc3[p][0:32, :], ALU.subtract).then_inc(r1_ok, 1)
                        for c in range(NH):
                            ins = pool.tensor_scalar(ud[:, c, :], u[:, c, :], parc[:, 6 + c:7 + c], 1.0, ALU.mult, ALU.mult)
                        ins.then_inc(ud_ok, 1)
                WHAT = {1: "rstd", 9: "r1"}

                def first():
                    for k in sorted(WHAT):
                        pre(-1, WHAT[k], 0)

                def body(i, p, prev, more):
                    for k in range(NS):
                        n = NS * i + k
                        pool.wait_ge(scan, CR + n + 1)
                        pool.wait_ge(ccp, CR + n + 1)
                        at_least(pool, red, CR + n + 1 - NGB)
                        pool.tensor_tensor(gg[k % NGB][:, :, :], hh[k % NHB][:, :, :], crs[k % NCS][:, :].unsqueeze(1).broadcast_to([128, NH, TOK]), ALU.mult).then_inc(prod, 1)
                        if more and k in WHAT:
                            pre(i, WHAT[k], 1 - p)

                loop(pool, body, first, lambda: None)


def store_phase(nc, K, out):
    sem = nc.semaphore("dbg_out")
    with sem as so:
        with nc.Block() as block:
            @block.sync
            def _(sp):
                sp.dma_start(out.rearrange("b t d -> t b d"), K["h_res"][:, :, :]).then_inc(so, 16)
                sp.wait_ge(so, 16)


def dense_phase(nc, A, K, x1_sb):
    ctx = ExitStack()
    with ctx:
        def sb(name, shape, dt=f32):
            return ctx.enter_context(nc.sbuf_tensor(name, shape, dt))

        def sem(name):
            return ctx.enter_context(nc.semaphore("d_" + name))

        NST = NE1 * NF
        NXW, NSG, NAC = 3, 3, 3
        DLAG = 2
        wgu, wbc, h_res, ident = K["wgu"], K["wbc"], K["h_res"], K["ident"]
        wdn = sb("wdn", [128, NE1, NF, D])
        xin = [sb(f"xin{p}", [128, G, D]) for p in range(2)]
        x1g = sb("x1g", [128, G, D])
        x1T = [sb(f"x1T{p}", [128, G, T]) for p in range(2)]
        xw = [sb(f"xw{b}", [128, G, T]) for b in range(NXW)]
        sg = [sb(f"sg{b}", [128, TOK]) for b in range(NSG)]
        ac = [sb(f"ac{b}", [128, TOK]) for b in range(NAC)]
        cT = sb("cT", [128, TOK])
        zrow = sb("zrow", [128, NSLOT * D // 128 // 8])
        bank = [ctx.enter_context(nc.psum_tensor(f"d_bank{b}", [128, 512], f32)) for b in range(8)]
        psG, psU, psD, psT, psM = bank[0:2], bank[2:4], bank[4], bank[5], bank[6:8]
        names = "w_ld sh_ld x_ld0 x_ld1 zero zeroed x1 trans xT scaled gated upped silued acted summed sum_ok logits tokens log_ok tok_ok".split()
        Q = {n: sem(n) for n in names}
        w_ld, zero, zeroed, x1_ok, trans, xT_ok, scaled, gated, upped, silued, acted, summed, sum_ok, logits, tokens, log_ok, tok_ok = (
            Q[n] for n in ("w_ld zero zeroed x1 trans xT scaled gated upped silued acted summed sum_ok logits tokens log_ok tok_ok").split())
        x_ld = [Q["x_ld0"], Q["x_ld1"]]

        def at_least(eng, sm, v):
            if not (isinstance(v, int) and v <= CR):
                eng.wait_ge(sm, v)

        def loop(eng, first, body):
            first()
            with eng.Fori(0, NG // 2 - 1) as j:
                body(2 * j, 0, True)
                body(2 * j + 1, 1, True)
            body(NG - 2, 0, True)
            body(NG - 1, 1, False)

        with nc.Block() as block:
            @block.sync
            def _(sp):
                def load_x(j, p):
                    at_least(sp, x1_ok, CR + 2 * j + p - 1)
                    sp.dma_start(xin[p][:, :, :], A["x"][ds((2 * j + p) * G, G), :, :].rearrange("b t d -> t b d")).then_inc(x_ld[p], 16)

                load_x(0, 0)
                load_x(0, 1)
                for e in range(NE):
                    sp.dma_start(wdn[:, e, :, :], A["Wd"][e].rearrange("(t p) d -> p t d", p=128)).then_inc(w_ld, 16)
                sp.dma_start(wdn[:, NE, :, :], A["Sd"].rearrange("(t p) d -> p t d", p=128)).then_inc(w_ld, 16)
                with sp.Fori(1, NG // 2) as j:
                    load_x(j, 0)
                    load_x(j, 1)
                sp.wait_ge(zero, 1)
                for c in range(8):
                    sp.dma_start(A["disp"].rearrange("(c p n) d -> c p (n d)", c=8, p=128)[c], zrow[:, :]).then_inc(zeroed, 16)
                sp.wait_ge(zeroed, 16 * 8)

            @block.gpsimd
            def _(pool):
                pool.sem_inc(scaled, CR)
                pool.memset(zrow[:, :], 0.0).then_inc(zero, 1)

                def body(g, p):
                    for e in range(NE1):
                        m = NE1 * g + e
                        if e == 0:
                            pool.wait_ge(xT_ok, CR + g + 1)
                        at_least(pool, upped, CR + NF * (m - NXW) + NF)
                        pool.tensor_tensor(xw[(NE1 * p + e) % NXW][:, :, :], x1T[p][:, :, :],
                                           wbc[:, e, ds(G * g, G)].unsqueeze(2).broadcast_to([128, G, T]), ALU.mult).then_inc(scaled, 1)

                body(0, 0)
                body(1, 1)
                with pool.Fori(1, NG // 2) as j:
                    body(2 * j, 0)
                    body(2 * j + 1, 1)

            @block.tensor
            def _(pe):
                for sm in (trans, gated, upped, summed, logits, tokens):
                    pe.sem_inc(sm, CR)

                def transpose_x(g):
                    pe.wait_ge(x1_ok, CR + g + 1)
                    at_least(pe, xT_ok, CR + g)
                    for q in range(G):
                        ins = pe.transpose(psT[:, q * T:(q + 1) * T], x1g[:, q, :], ident[:, :])
                    ins.then_inc(trans, 1)

                def down(g, p, r):
                    n = NST * g + r
                    if r == 0:
                        at_least(pe, sum_ok, CR + g)
                    pe.wait_ge(acted, CR + n + 1)
                    ins = pe.matmul(psD[:, :], lhsT=wdn[:, r // NF, r % NF, :], rhs=ac[r % NAC][:, :], start=(r == 0), stop=(r == NST - 1))
                    ins.then_inc(summed, 1)

                def post(g):
                    pe.wait_ge(sum_ok, CR + g + 1)
                    at_least(pe, log_ok, CR + g)
                    for q in range(G):
                        ins = pe.matmul(psM[0][:, q * NE:(q + 1) * NE], lhsT=cT[:, q * T:(q + 1) * T], rhs=K["wr"][:, :], start=True, stop=True)
                    ins.then_inc(logits, 1)
                    at_least(pe, tok_ok, CR + g)
                    for q in range(G):
                        ins = pe.transpose(psM[1][:, q * T:(q + 1) * T], cT[:, q * T:(q + 1) * T], ident[:, :])
                    ins.then_inc(tokens, 1)

                def body(g, p, more, prev=True):
                    for r in range(NST):
                        n = NST * g + r
                        e, f = r // NF, r % NF
                        if r == 0:
                            pe.wait_ge(xT_ok, CR + g + 1)
                        at_least(pe, silued, CR + n - 1)
                        pe.matmul(psG[r % 2][:, :], lhsT=wgu[:, e, 0, f * 128:(f + 1) * 128], rhs=x1T[p][:, :, :], start=True, stop=True).then_inc(gated, 1)
                        if f == 0:
                            pe.wait_ge(scaled, CR + NE1 * g + e + 1)
                        at_least(pe, acted, CR + n - 1)
                        pe.matmul(psU[r % 2][:, :], lhsT=wgu[:, e, 1, f * 128:(f + 1) * 128], rhs=xw[(NE1 * p + e) % NXW][:, :, :], start=True, stop=True).then_inc(upped, 1)
                        if r >= DLAG:
                            down(g, p, r - DLAG)
                        if more and r == 12:
                            transpose_x(g + 1)
                    for r in range(NST - DLAG, NST):
                        down(g, p, r)
                    post(g)

                def first():
                    transpose_x(0)
                    pe.wait_ge(w_ld, 16 * NE1)

                loop(pe, first, body)

            @block.scalar
            def _(act):
                for sm in (xT_ok, silued, sum_ok, tok_ok):
                    act.sem_inc(sm, CR)

                def copy_x(g, p):
                    act.wait_ge(trans, CR + g + 1)
                    at_least(act, upped, CR + NST * (g - 1))
                    act.activation(x1T[p][:, :, :].rearrange("p q t -> p (q t)"), psT[:, :], ACT.Copy).then_inc(xT_ok, 1)

                def body(g, p, more):
                    for r in range(NST):
                        n = NST * g + r
                        act.wait_ge(gated, CR + n + 1)
                        at_least(act, acted, CR + n + 1 - NSG)
                        act.activation(sg[r % NSG][:, :], psG[r % 2][:, :], ACT.Silu).then_inc(silued, 1)
                        if more and r == 14:
                            copy_x(g + 1, 1 - p)
                    act.wait_ge(summed, CR + NST * (g + 1))
                    at_least(act, tokens, CR + g)
                    act.activation(cT[:, :], psD[:, :], ACT.Copy).then_inc(sum_ok, 1)
                    act.wait_ge(tokens, CR + g + 1)
                    act.activation(h_res[:, ds(g * G, G), :].rearrange("p q d -> p (q d)"), psM[1][:, :], ACT.Copy).then_inc(tok_ok, 1)

                loop(act, lambda: copy_x(0, 0), body)

            @block.vector
            def _(dve):
                for sm in (x1_ok, acted, log_ok):
                    dve.sem_inc(sm, CR)

                def residual(g, p):
                    at_least(dve, trans, CR + g)
                    dve.wait_ge(x_ld[p], 16 * (g // 2 + 1) if isinstance(g, int) else 8 * (g - p + 2))
                    dve.tensor_tensor(x1g[:, :, :], xin[p][:, :, :], h_res[:, ds(g * G, G), :], ALU.add)
                    dve.tensor_tensor(x1_sb[:, ds(g * G, G), :], xin[p][:, :, :], h_res[:, ds(g * G, G), :], ALU.add).then_inc(x1_ok, 1)

                def body(g, p, more):
                    for r in range(NST):
                        n = NST * g + r
                        if more and r == 4:
                            residual(g + 1, 1 - p)
                        dve.wait_ge(silued, CR + n + 1)
                        dve.wait_ge(upped, CR + n + 1)
                        at_least(dve, summed, CR + n + 1 - NAC)
                        dve.tensor_tensor(ac[r % NAC][:, :], sg[r % NSG][:, :], psU[r % 2][:, :], ALU.mult).then_inc(acted, 1)
                    dve.wait_ge(logits, CR + g + 1)
                    dve.tensor_copy(K["lg"][:, ds(g * G, G), :].rearrange("p q e -> p (q e)"), psM[0][:, 0:G * NE]).then_inc(log_ok, 1)

                loop(dve, lambda: residual(0, 0), body)


def router_phase(nc, A, K):
    ctx = ExitStack()
    with ctx:
        def sb(name, shape, dt=f32):
            return ctx.enter_context(nc.sbuf_tensor(name, shape, dt))

        all_e = [128, NSEQ, NE]
        lg = K["lg"]
        gates, m1, m2, l2, tmp, score, pos, tot, cum = (sb("r_" + n, all_e) for n in "gates m1 m2 l2 tmp score pos tot cum".split())
        mx, den, g1, g2, s1, s2, b1, b2, keep = (sb("r_" + n, [128, NSEQ]) for n in "mx den g1 g2 s1 s2 b1 b2 keep".split())
        rank = sb("r_rank", [128, NE])
        base = sb("r_base", [128, NE])
        one_t = sb("r_one_t", [128, NSEQ])
        tri = sb("tri", [128, 128])
        ones = sb("ones", [128, 128])
        psP = ctx.enter_context(nc.psum_tensor("r_psP", [128, 512], f32))
        psS = ctx.enter_context(nc.psum_tensor("r_psS", [128, 512], f32))
        made, chain, expd, masked, counted, pch = (ctx.enter_context(nc.semaphore("r_" + n)) for n in "made chain expd masked counted pch".split())

        def over_e(v):
            return v[:, :].unsqueeze(2).broadcast_to(all_e)

        def over_t(v):
            return v[:, :].unsqueeze(1).broadcast_to(all_e)

        with nc.Block() as block:
            @block.gpsimd
            def _(pool):
                n = 0

                def link(ins):
                    nonlocal n
                    n += 1
                    ins.then_inc(pch, 1)
                    pool.wait_ge(pch, n)

                link(pool.memset(ones[:, :], 1.0))
                link(pool.memset(one_t[:, :], 1.0))
                link(pool.affine_select(out=tri[:, :], in_=ones[:, :], compare_op=ALU.is_gt, fill=0.0, base=0, pattern=[[1, 128]], channel_multiplier=-1))
                for e in range(NE):
                    pool.memset(rank[:, e:e + 1], float(NE - e))
                    ins = pool.memset(base[:, e:e + 1], float(e * CAP))
                ins.then_inc(made, 1)

            @block.scalar
            def _(act):
                act.wait_ge(masked, 1)
                act.activation(gates[:, :, :], tmp[:, :, :], ACT.Exp).then_inc(expd, 1)

            @block.tensor
            def _(pe):
                for c, m in ((0, m1), (1, m2)):
                    pe.wait_ge(masked, 2 + c)
                    if c == 0:
                        pe.wait_ge(made, 1)
                    else:
                        pe.wait_ge(counted, 2)
                    pe.matmul(psP[:, 0:NSEQ * NE], lhsT=tri[:, :], rhs=m[:, :, :].rearrange("p b e -> p (b e)"), start=True, stop=True)
                    pe.matmul(psS[:, 0:NSEQ * NE], lhsT=ones[:, :], rhs=m[:, :, :].rearrange("p b e -> p (b e)"), start=True, stop=True).then_inc(counted, 1)

            @block.vector
            def _(dve):
                n = 0

                def link(ins):
                    nonlocal n
                    n += 1
                    ins.then_inc(chain, 1)
                    dve.wait_ge(chain, n)

                def tt(o, a, b, op):
                    link(dve.tensor_tensor(o, a, b, op))

                def reduced(o, a, op):
                    link(dve.tensor_reduce(o, a, AX.X, op))

                def first_of(m, vals, best):
                    tt(tmp[:, :, :], vals, over_e(best), ALU.is_equal)
                    tt(score[:, :, :], tmp[:, :, :], over_t(rank), ALU.mult)
                    reduced(keep[:, :], score[:, :, :], ALU.max)
                    tt(m, score[:, :, :], over_e(keep), ALU.is_equal)

                dve.wait_ge(made, 1)
                reduced(mx[:, :], lg[:, :, :], ALU.max)
                dve.tensor_tensor(tmp[:, :, :], lg[:, :, :], over_e(mx), ALU.subtract).then_inc(masked, 1)
                dve.wait_ge(expd, 1)
                reduced(den[:, :], gates[:, :, :], ALU.add)
                link(dve.reciprocal(den[:, :], den[:, :]))
                tt(gates[:, :, :], gates[:, :, :], over_e(den), ALU.mult)
                reduced(mx[:, :], gates[:, :, :], ALU.max)
                first_of(m1[:, :, :], gates[:, :, :], mx)
                link(dve.tensor_scalar(l2[:, :, :], m1[:, :, :], -3.0e38, None, ALU.mult))
                dve.tensor_tensor(l2[:, :, :], l2[:, :, :], lg[:, :, :], ALU.add).then_inc(masked, 1)
                dve.wait_ge(masked, 2)
                reduced(mx[:, :], l2[:, :, :], ALU.max)
                first_of(m2[:, :, :], l2[:, :, :], mx)
                tt(tmp[:, :, :], gates[:, :, :], m1[:, :, :], ALU.mult)
                reduced(g1[:, :], tmp[:, :, :], ALU.add)
                dve.tensor_tensor(tmp[:, :, :], gates[:, :, :], m2[:, :, :], ALU.mult).then_inc(masked, 1)
                dve.wait_ge(masked, 3)
                reduced(g2[:, :], tmp[:, :, :], ALU.add)
                tt(den[:, :], g1[:, :], g2[:, :], ALU.add)
                link(dve.tensor_scalar(den[:, :], den[:, :], 1e-9, None, ALU.max))
                link(dve.reciprocal(den[:, :], den[:, :]))
                tt(g1[:, :], g1[:, :], den[:, :], ALU.mult)
                tt(g2[:, :], g2[:, :], den[:, :], ALU.mult)
                for c, (m, g, w) in enumerate(((m1, g1, K["w1"]), (m2, g2, K["w2"]))):
                    dve.wait_ge(counted, 2 * c + 1)
                    link(dve.tensor_copy(tot[:, :, :].rearrange("p b e -> p (b e)"), psS[:, 0:NSEQ * NE]))
                    for e in range(NE):
                        start = 0.0 if c == 0 else s2[:, e:e + 1]
                        ins = dve.tensor_tensor_scan(out=cum[:, :, e], data0=one_t[:, :], data1=tot[:, :, e], initial=start, op0=ALU.mult, op1=ALU.add)
                    link(ins)
                    tt(pos[:, :, :], cum[:, :, :], tot[:, :, :], ALU.subtract)
                    link(dve.tensor_copy(s2[:, 0:NE], cum[:, NSEQ - 1, :]))
                    dve.tensor_tensor(pos[:, :, :], pos[:, :, :], psP[:, 0:NSEQ * NE].rearrange("p (b e) -> p b e", e=NE), ALU.add).then_inc(counted, 1)
                    dve.wait_ge(counted, 2 * c + 2)
                    tt(tmp[:, :, :], pos[:, :, :], m[:, :, :], ALU.mult)
                    reduced(s1[:, :], tmp[:, :, :], ALU.add)
                    tt(tmp[:, :, :], m[:, :, :], over_t(base), ALU.mult)
                    reduced(b1[:, :], tmp[:, :, :], ALU.add)
                    link(dve.tensor_scalar(keep[:, :], s1[:, :], float(CAP), None, ALU.is_lt))
                    tt(w[:, :], g[:, :], keep[:, :], ALU.mult)
                    link(dve.scalar_tensor_tensor(out=b1[:, :], in0=s1[:, :], scalar=float(CAP - 1), in1=b1[:, :], op0=ALU.min, op1=ALU.add))
                    link(dve.tensor_copy(K["gather"][c][:, :], b1[:, :]))
                    link(dve.tensor_scalar(b2[:, :], keep[:, :], -FAR, FAR, ALU.mult, ALU.add))
                    tt(b1[:, :], b1[:, :], b2[:, :], ALU.add)
                    link(dve.tensor_copy(K["scatter"][c][:, :], b1[:, :]))


def sparse_phase(nc, A, K, x1_sb, out):
    ctx = ExitStack()
    with ctx:
        def sb(name, shape, dt=f32):
            return ctx.enter_context(nc.sbuf_tensor(name, shape, dt))

        def sem(name):
            return ctx.enter_context(nc.semaphore("e_" + name))

        NO = 4
        NHT = CAP // 512
        wg = [sb(f"ewg{p}", [128, F]) for p in range(2)]
        wd = [sb(f"ewd{p}", [128, NF, D]) for p in range(2)]
        dx = [sb(f"dx{p}", [128, NCH, D]) for p in range(2)]
        dT = [sb(f"dT{b}", [128, 512]) for b in range(2)]
        ht = [sb(f"ht{b}", [128, NF, 512]) for b in range(2)]
        eos = [sb(f"eos{p}", [128, NCH, D]) for p in range(2)]
        got = [[sb(f"got{c}_{b}", [128, D]) for b in range(NO)] for c in range(2)]
        part = [sb(f"part{b}", [128, D]) for b in range(NO)]
        fin = [sb(f"fin{b}", [128, D]) for b in range(NO)]
        bank = [ctx.enter_context(nc.psum_tensor(f"e_bank{b}", [128, 512], f32)) for b in range(8)]
        psT, psH, psE = bank[0:2], bank[2:6], bank[6:8]
        w_ld, x_ld = [sem("w_ld0"), sem("w_ld1")], [sem("x_ld0"), sem("x_ld1")]
        sct = sem("sct")
        trans, copied, upped, gelud, downed, evac, stored = (sem(n) for n in "trans copied upped gelud downed evac stored".split())
        gat = [sem(f"gat{b}") for b in range(NO)]
        outs = [sem(f"outs{b}") for b in range(NO)]
        partd, find = sem("partd"), sem("find")
        disp, eo = A["disp"], A["eo"]

        def at_least(eng, sm, v):
            if not (isinstance(v, int) and v <= CR):
                eng.wait_ge(sm, v)

        def experts(eng, body):
            with eng.Fori(0, NE // 2) as j:
                body(2 * j, 0, j)
                body(2 * j + 1, 1, j)

        with nc.Block() as block:
            @block.sync
            def _(sp):
                sp.sem_inc(stored, 16)

                def load(e, p):
                    at_least(sp, evac, CR + NHT * (e - 1))
                    sp.dma_start(wg[p][:, :], A["w_gate"][ds(e, 1), :, :].rearrange("o d f -> (o d) f")).then_inc(w_ld[p], 16)
                    sp.dma_start(wd[p][:, :, :], A["w_down"][ds(e, 1), :, :].rearrange("o (t p) d -> p (o t) d", p=128)).then_inc(w_ld[p], 16)
                    if isinstance(e, int) and e == 0:
                        sp.wait_ge(sct, 16 * 2 * NSEQ)
                    sp.dma_start(dx[p][:, :, :], disp[ds(e * CAP, CAP), :].rearrange("(c p) d -> p c d", p=128)).then_inc(x_ld[p], 16)

                def store(e, p):
                    sp.wait_ge(evac, CR + NHT * (e + 1))
                    sp.dma_start(eo[ds(e * CAP, CAP), :].rearrange("(c p) d -> p c d", p=128), eos[p][:, :, :]).then_inc(stored, 16)

                load(0, 0)
                load(1, 1)
                with sp.Fori(0, NE // 2 - 1) as j:
                    store(2 * j, 0)
                    load(2 * j + 2, 0)
                    store(2 * j + 1, 1)
                    load(2 * j + 3, 1)
                store(NE - 2, 0)
                store(NE - 1, 1)
                for b in range(NSEQ):
                    sp.wait_ge(find, b + 1)
                    sp.dma_start(out[b], fin[b % NO][:, :]).then_inc(outs[b % NO], 16)
                for b in range(NO):
                    sp.wait_ge(outs[b], 16 * NSEQ // NO)

            @block.gpsimd
            def _(pool):
                for b in range(NSEQ):
                    for c in range(2):
                        pool.indirect_dma_start(disp, bass.IndirectOffsetOnAxis(ap=K["scatter"][c][:, b:b + 1], axis=0),
                                                K["h_res"][:, b, :], None, bounds_check=NSLOT - 1, oob_is_err=False).then_inc(sct, 16)
                pool.wait_ge(stored, 16 + 16 * NE)
                for b in range(NSEQ):
                    if b >= NO:
                        pool.wait_ge(find, b + 1 - NO)
                    for c in range(2):
                        pool.indirect_dma_start(got[c][b % NO][:, :], None, eo,
                                                bass.IndirectOffsetOnAxis(ap=K["gather"][c][:, b:b + 1], axis=0)).then_inc(gat[b % NO], 16)

            @block.tensor
            def _(pe):
                for sm in (trans, upped, downed):
                    pe.sem_inc(sm, CR)

                def up(e, p, j, c):
                    h = NHT * e + c
                    if c == 0:
                        pe.wait_ge(x_ld[p], 16 * (j + 1))
                        pe.wait_ge(w_ld[p], 32 * (j + 1))
                    at_least(pe, copied, CR + h - 1)
                    for q in range(4):
                        ins = pe.transpose(psT[c][:, q * 128:(q + 1) * 128], dx[p][:, 4 * c + q, :], K["ident"][:, :])
                    ins.then_inc(trans, 1)
                    pe.wait_ge(copied, CR + h + 1)
                    for f in range(NF):
                        at_least(pe, gelud, CR + NF * (h - 1) + f + 1)
                        pe.matmul(psH[f][:, :], lhsT=wg[p][:, f * 128:(f + 1) * 128], rhs=dT[c][:, :], start=True, stop=True).then_inc(upped, 1)

                def down(e, p, c):
                    h = NHT * e + c
                    pe.wait_ge(gelud, CR + NF * (h + 1))
                    at_least(pe, evac, CR + h - 1)
                    for q in range(4):
                        for f in range(NF):
                            ins = pe.matmul(psE[c][:, q * 128:(q + 1) * 128], lhsT=ht[c][:, f, q * 128:(q + 1) * 128], rhs=wd[p][:, f, :], start=(f == 0), stop=(f == NF - 1))
                    ins.then_inc(downed, 1)

                def body(e, p, j):
                    up(e, p, j, 0)
                    up(e, p, j, 1)
                    down(e, p, 0)
                    down(e, p, 1)

                experts(pe, body)

            @block.scalar
            def _(act):
                act.sem_inc(gelud, CR)

                def body(e, p, j):
                    for c in range(NHT):
                        h = NHT * e + c
                        at_least(act, downed, CR + h - 1)
                        for f in range(NF):
                            act.wait_ge(upped, CR + NF * h + f + 1)
                            act.activation(ht[c][:, f, :], psH[f][:, :], ACT.Gelu).then_inc(gelud, 1)

                experts(act, body)

            @block.vector
            def _(dve):
                dve.sem_inc(copied, CR)
                dve.sem_inc(evac, CR)

                def body(e, p, j):
                    for c in range(NHT):
                        h = NHT * e + c
                        dve.wait_ge(trans, CR + h + 1)
                        at_least(dve, upped, CR + NF * (h - 1))
                        dve.tensor_copy(dT[c][:, :], psT[c][:, :]).then_inc(copied, 1)
                    for c in range(NHT):
                        h = NHT * e + c
                        dve.wait_ge(downed, CR + h + 1)
                        dve.wait_ge(stored, 16 + 16 * (e - 1))
                        dve.tensor_copy(eos[p][:, 4 * c:4 * c + 4, :].rearrange("p q d -> p (q d)"), psE[c][:, :]).then_inc(evac, 1)

                experts(dve, body)
                for b in range(NSEQ):
                    dve.wait_ge(gat[b % NO], 32 * (b // NO + 1))
                    dve.scalar_tensor_tensor(out=part[b % NO][:, :], in0=got[0][b % NO][:, :], scalar=K["w1"][:, b:b + 1], in1=x1_sb[:, b, :], op0=ALU.mult, op1=ALU.add).then_inc(partd, 1)
                    dve.wait_ge(partd, b + 1)
                    if b >= NO:
                        dve.wait_ge(outs[b % NO], 16 * (b // NO))
                    dve.scalar_tensor_tensor(out=fin[b % NO][:, :], in0=got[1][b % NO][:, :], scalar=K["w2"][:, b:b + 1], in1=part[b % NO][:, :], op0=ALU.mult, op1=ALU.add).then_inc(find, 1)


def mega(nc, A, out, stop=0):
    ctx = ExitStack()
    with ctx:
        def sb(c, name, shape, dt=f32):
            return c.enter_context(nc.sbuf_tensor(name, shape, dt))

        K = {
            "h_res": sb(ctx, "h_res", [128, NSEQ, D]),
            "ident": sb(ctx, "ident", [128, 128]),
            "eps": sb(ctx, "eps", [128, G]),
            "nhalf": sb(ctx, "nhalf", [128, G]),
            "wgu": sb(ctx, "wgu", [128, NE1, 2, F]),
            "wbc": sb(ctx, "wbc", [128, NE1, NSEQ]),
            "sgp": sb(ctx, "sgp", [128, NSEQ]),
            "wr": sb(ctx, "wr", [128, NE]),
        }
        with ExitStack() as c2:
            M = {
                "taps": sb(c2, "taps", [128, NL, NTAP, DI]),
                "wz": sb(c2, "wz", [128, NL, DI]),
                "wx": sb(c2, "wx", [128, NL * NH, NX]),
                "wdt": sb(c2, "wdt", [64, NL, DI]),
                "wo": sb(c2, "wo", [128, NL * NH, D]),
                "par": sb(c2, "par", [128, NL, 8]),
                "negA": sb(c2, "negA", [128, NL, NH * NS]),
                "sel": sb(c2, "sel", [96, 2 * NS, 128], bf16),
                "xnT": sb(c2, "xnT", [128, G, T + NTAP - 1]),
            }
            M["zpad"] = M["xnT"][:, :, 0:NTAP - 1]
            setup_phase(nc, A, K, M)
            if stop != 1:
                mamba_phase(nc, A, K, M)
        if stop in (1, 2):
            store_phase(nc, K, out)
            return
        with ExitStack() as c5:
            x1_sb = sb(c5, "x1_sb", [128, NSEQ, D])
            K["lg"] = sb(c5, "lg", [128, NSEQ, NE])
            K["w1"], K["w2"] = sb(c5, "gw1", [128, NSEQ]), sb(c5, "gw2", [128, NSEQ])
            K["scatter"] = [sb(c5, f"scatter{c}", [128, NSEQ], u32) for c in range(2)]
            K["gather"] = [sb(c5, f"gather{c}", [128, NSEQ], u32) for c in range(2)]
            dense_phase(nc, A, K, x1_sb)
            if stop == 3:
                store_phase(nc, K, out)
                return
            router_phase(nc, A, K)
            sparse_phase(nc, A, K, x1_sb, out)


STOP = 0


def kernel(**inputs):
    import numpy as np
    import concourse.bacc as bacc
    from concourse.bass_utils import run_bass_kernel_spmd

    I = {k: np.asarray(v) for k, v in inputs.items()}
    c = np.ascontiguousarray

    def halves(a):
        return a.reshape(NL, NH, 128).transpose(2, 0, 1)

    perm = list(range(DTR, NX)) + list(range(DTR))
    par = np.concatenate([I["L0_attn_ln_w"].T[:, :, None], I["L0_attn_ln_b"].T[:, :, None], halves(I["L0_attn_conv_b"]),
                          halves(I["L0_attn_b_dt"]), halves(I["L0_attn_Dp"])], axis=2)
    arrays = {
        "x": I["x"], "ids": I["itok_B_0_8"].reshape(1, NSEQ), "gateT": I["fside_Bx8_0"].T, "sgate": I["condB_sharedgateprob"].reshape(1, NSEQ),
        "W1": I["L0_cond_W1"], "b1": I["L0_cond_b1"], "W2": I["L0_cond_W2"], "b2": I["L0_cond_b2"],
        "gamma": I["L0_cond_gamma"], "beta": I["L0_cond_beta"],
        "W_inT": I["L0_attn_W_in"].transpose(0, 2, 1), "conv_wT": I["L0_attn_conv_w"].transpose(0, 2, 1),
        "W_xT": I["L0_attn_W_x"][:, perm, :].transpose(0, 2, 1), "W_dtT": I["L0_attn_W_dt"].transpose(0, 2, 1),
        "W_outT": I["L0_attn_W_out"].transpose(0, 2, 1), "par": par,
        "A_log": I["L0_attn_A_log"].reshape(NL, NH, 128, NS).transpose(2, 0, 1, 3).reshape(128, NL, NH * NS),
        "Wg": I["L0_cond2_Wg"], "Wu": I["L0_cond2_Wu"], "Wd": I["L0_cond2_Wd"],
        "Sg": I["L0_cond2_Sg"], "Su": I["L0_cond2_Su"], "Sd": I["L0_cond2_Sd"],
        "wg": I["L0_ffn_wg"], "w_gate": I["L0_ffn_w_gate"], "w_down": I["L0_ffn_w_down"],
    }
    nc = bacc.Bacc("TRN2", target_bir_lowering=False, num_devices=1)
    arrays = {f"in_{k}": c(v) for k, v in arrays.items()}
    A = {k[3:]: nc.dram_tensor(k, v.shape, mybir.dt.from_np(v.dtype), kind="ExternalInput").ap() for k, v in arrays.items()}
    A["disp"] = nc.dram_tensor("disp", (NSLOT, D), f32, kind="Internal").ap()
    A["eo"] = nc.dram_tensor("eo", (NSLOT, D), f32, kind="Internal").ap()
    out = nc.dram_tensor("out", (NSEQ, T, D), f32, kind="ExternalOutput").ap()
    mega(nc, A, out, STOP)
    r = run_bass_kernel_spmd(nc, [arrays], core_ids=[0])
    return r.results[0]["out"]
```

```python
import concourse.bass as bass
from concourse import mybir
from contextlib import ExitStack

NSEQ, T, D = 32, 128, 128
NL, DI, NS, NTAP = 4, 256, 16, 4
DTR = 8
NX = 2 * NS + DTR
G = 4
NG = NSEQ // G
TOK = G * T
NH = DI // 128
NIT = NL * NG
ADP, NLANG = 32, 10
NE, F, NF = 8, 512, 4
NE1 = NE + 1
CAP = 2 * NSEQ * T // NE
NSLOT = NE * CAP
NCH = CAP // 128
EPS = 1e-5
CR = 8
NDA, NDB, NHB, NGB, NCS = 4, 2, 2, 4, 4
RLAG = 3
WUSE = 9
OUTP = 4
CLEAD = 2
PE_AT = {1: ["x0"], 2: ["more_x0"], 3: ["x1"], 4: ["more_x1"], 5: ["z0"], 6: ["z1"], 9: ["bcdt"], 10: ["dt0"], 11: ["dt1"]}
ACT_AT = {1: ["params", "norm"], 4: ["x0"], 5: ["x1"], 6: ["z0"], 7: ["z1"], 9: ["silu"], 11: ["bcdt"], 12: ["dt0"], 13: ["dt1"], 14: ["mid"],
          15: ["softplus"]}
DVE_AT = {4: ["gate"], 9: ["residual", "moments"], 10: ["diag"], 12: ["lo"], 13: ["abs"], 14: ["centre"], 15: ["dt"]}
PAIRED = (2, 15)
OUT_AT, SKIP_AT, TR_AT, RSTD_AT, R1_AT = 7, 12, 15, 12, 11
LNEXP = "natural_log_exp_and_others"
FAR = 65536.0

f32, bf16, i32, u32 = mybir.dt.float32, mybir.dt.bfloat16, mybir.dt.int32, mybir.dt.uint32
ALU, ACT, AX = mybir.AluOpType, mybir.ActivationFunctionType, mybir.AxisListType
ds = bass.ds


def setup_phase(nc, A, K, M):
    ctx = ExitStack()
    with ctx:
        def sb(name, shape, dt=f32):
            return ctx.enter_context(nc.sbuf_tensor(name, shape, dt))

        def sem(name):
            return ctx.enter_context(nc.semaphore(name))

        NAB = 4
        ids = sb("ids", [1, NSEQ], i32)
        xg = [sb(f"xg{p}", [128, G, D]) for p in range(NAB)]
        w12 = [sb(f"ad_w12{p}", [128, G, ADP + D + 1]) for p in range(NAB)]
        gb = [sb(f"ad_gb{p}", [128, G, 2, D]) for p in range(NAB)]
        xT = sb("ad_xT", [128, TOK])
        hT = sb("ad_hT", [64, TOK])
        y = sb("ad_y", [128, G, D])
        nrm = sb("ad_nrm", [128, G, D])
        stats = sb("ad_stats", [128, G, 6])
        mv = sb("ad_mv", [128, G, 2])
        vare = sb("ad_vare", [128, G])
        rstd = sb("ad_rstd", [128, G])
        spare = sb("ad_spare", [128, 1])
        wraw = sb("wraw", [128, NL, DI])
        cwb = sb("cwb", [128, NL * NTAP * DI])
        psT = ctx.enter_context(nc.psum_tensor("ad_psT", [128, 512], f32))
        psH = ctx.enter_context(nc.psum_tensor("ad_psH", [128, 512], f32))
        psA = ctx.enter_context(nc.psum_tensor("ad_psA", [128, 512], f32))

        ids_ld, raw_ld, w_ld, moe_ld, ad_ld = sem("ids_ld"), sem("raw_ld"), sem("w_ld"), sem("moe_ld"), [sem(f"ad_ld{p}") for p in range(NAB)]
        cst, tapped, xTd, xTc, hTd, hTc, summed = (sem(n) for n in ("cst", "tapped", "xTd", "xTc", "hTd", "hTc", "summed"))
        ysum, stat, var_ok, rstd_ok, normed, placed, pch, a_ok = (
            sem(n) for n in ("ysum", "stat", "var_ok", "rstd_ok", "normed", "placed", "pch", "a_ok"))
        NAD = 1 + 2 * G

        with nc.Block() as block:
            @block.sync
            def _(sp):
                sp.dma_start(ids[:, :], A["ids"]).then_inc(ids_ld, 16)
                sp.wait_ge(ids_ld, 16)
                sp.sem_inc(placed, CR)

                def load(j, p):
                    g = NAB * j + p
                    sp.wait_ge(placed, CR + g + 1 - NAB)
                    sp.dma_start(xg[p][:, :, :], A["x"][ds(g * G, G), :, :].rearrange("b t d -> t b d")).then_inc(ad_ld[p], 16)
                    for q in range(G):
                        lid = sp.value_load(ids[0:1, ds(g * G + q, 1)], min_val=0, max_val=NLANG - 1)
                        one = ds(lid, 1)
                        sp.dma_start(w12[p][:, q, :], A["W12"][one, :, :].rearrange("o h a -> (o h) a")).then_inc(ad_ld[p], 16)
                        sp.dma_start(gb[p][:, q, :, :], A["gb"][one, :, :].broadcast_to([128, 2, D])).then_inc(ad_ld[p], 16)

                with sp.Fori(0, NG // NAB) as j:
                    for p in range(NAB):
                        load(j, p)
                sp.dma_start(K["wgu"][:, 0:NE, 0, :], A["Wg"].rearrange("e d f -> d e f")).then_inc(K["wgu_ld"], 16)
                sp.dma_start(K["wgu"][:, 0:NE, 1, :], A["Wu"].rearrange("e d f -> d e f")).then_inc(K["wgu_ld"], 16)
                sp.dma_start(K["wgu"][:, NE, 0, :], A["Sg"]).then_inc(K["wgu_ld"], 16)
                sp.dma_start(K["wgu"][:, NE, 1, :], A["Su"]).then_inc(K["wgu_ld"], 16)

            @block.scalar
            def _(act):
                act.dma_start(wraw[:, :, :], A["W_inT"][:, :, 0:DI].rearrange("l m d -> m l d")).then_inc(raw_ld, 16)
                act.dma_start(cwb[:, :], A["conv_wT"].rearrange("l k d -> (l k d)").unsqueeze(0).broadcast_to([128, NL * NTAP * DI])).then_inc(raw_ld, 16)
                act.dma_start(M["negA"][:, :, :], A["A_log"]).then_inc(w_ld, 16)
                act.dma_start(M["wz"][:, :, :], A["W_inT"][:, :, DI:2 * DI].rearrange("l m d -> m l d")).then_inc(w_ld, 16)
                act.dma_start(M["wx"][:, :, :], A["W_xT"].rearrange("l (c p) r -> p (l c) r", p=128)).then_inc(w_ld, 16)
                act.dma_start(M["wdt"][32:32 + DTR, :, :], A["W_dtT"].rearrange("l r d -> r l d")).then_inc(w_ld, 16)
                act.dma_start(M["wo"][:, :, :], A["W_outT"].rearrange("l (c p) m -> p (l c) m", p=128)).then_inc(w_ld, 16)
                act.dma_start(M["par"][:, :, :], A["par"]).then_inc(w_ld, 16)
                act.dma_start(K["wbc"][:, 0:NE, :], A["gateT"].rearrange("e b -> (e b)").unsqueeze(0).broadcast_to([128, NE * NSEQ]).rearrange("p (e b) -> p e b", e=NE)).then_inc(moe_ld, 16)
                act.dma_start(K["sgp"][:, :], A["sgate"].broadcast_to([128, NSEQ])).then_inc(moe_ld, 16)
                act.dma_start(K["wr"][:, :], A["wg"]).then_inc(moe_ld, 16)
                act.sem_inc(xTc, CR)
                act.sem_inc(hTc, CR)
                act.wait_ge(w_ld, 16 * 6)
                act.activation(M["negA"][:, :, :], M["negA"][:, :, :], ACT.Exp).then_inc(a_ok, 1)

                def adapter(j, p):
                    g = NAB * j + p
                    act.wait_ge(xTd, CR + g + 1)
                    act.wait_ge(hTd, CR + g)
                    act.activation(xT[:, :], psT[:, :], ACT.Copy).then_inc(xTc, 1)
                    act.wait_ge(hTd, CR + g + 1)
                    act.wait_ge(summed, CR + g)
                    for q in range(G):
                        ins = act.activation(hT[0:ADP, q * T:(q + 1) * T], psH[0:ADP, q * T:(q + 1) * T], ACT.Relu, bias=w12[p][0:ADP, q, ADP + D:ADP + D + 1])
                    ins.then_inc(hTc, 1)

                with act.Fori(0, NG // NAB) as j:
                    for p in range(NAB):
                        adapter(j, p)
                act.wait_ge(moe_ld, 16 * 3)

            @block.gpsimd
            def _(pool):
                n = 0

                def link(ins):
                    nonlocal n
                    n += 1
                    ins.then_inc(pch, 1)
                    pool.wait_ge(pch, n)

                pool.sem_inc(rstd_ok, CR)
                link(pool.memset(K["ident"][:, :], 0.0))
                link(pool.affine_select(out=K["ident"][:, :], in_=K["ident"][:, :], compare_op=ALU.not_equal, fill=1.0,
                                        base=0, pattern=[[-1, 128]], channel_multiplier=1))
                link(pool.memset(K["eps"][:, :], EPS))
                link(pool.memset(K["nhalf"][:, :], -0.5))
                link(pool.memset(hT[32:33, :], 1.0))
                pool.memset(M["zpad"], 0.0).then_inc(cst, 1)
                link(pool.memset(M["sel"][:, :, :], 0.0))
                for q in range(3):
                    link(pool.affine_select(out=M["sel"][:, :, :], in_=M["sel"][:, :, :], compare_op=ALU.not_equal, fill=1.0,
                                            base=-32 * q, pattern=[[-1, 2 * NS], [0, 128]], channel_multiplier=1))
                pool.wait_ge(raw_ld, 32)
                for l in range(NL):
                    for k in range(NTAP):
                        pool.tensor_tensor(M["taps"][:, l, k, :], wraw[:, l, :], cwb[:, (l * NTAP + k) * DI:(l * NTAP + k + 1) * DI], ALU.mult)
                with pool.Fori(0, NG) as g:
                    pool.wait_ge(stat, CR + g + 1)
                    pool.tensor_tensor(vare[:, :], mv[:, :, 1], K["eps"][:, :], ALU.add).then_inc(var_ok, 1)
                    pool.wait_ge(var_ok, g + 1)
                    pool.tensor_tensor(rstd[:, :], vare[:, :], K["nhalf"][:, :], ALU.pow).then_inc(rstd_ok, 1)

            @block.tensor
            def _(pe):
                pe.sem_inc(xTd, CR)
                pe.sem_inc(hTd, CR)
                pe.sem_inc(summed, CR)
                pe.wait_ge(cst, 1)

                def adapter(j, p):
                    g = NAB * j + p
                    pe.wait_ge(ad_ld[p], 16 * NAD * (j + 1))
                    pe.wait_ge(xTc, CR + g)
                    for q in range(G):
                        ins = pe.transpose(psT[:, q * T:(q + 1) * T], xg[p][:, q, :], K["ident"][:, :])
                    ins.then_inc(xTd, 1)
                    pe.wait_ge(xTc, CR + g + 1)
                    pe.wait_ge(hTc, CR + g)
                    for q in range(G):
                        ins = pe.matmul(psH[0:ADP, q * T:(q + 1) * T], lhsT=w12[p][:, q, 0:ADP], rhs=xT[:, q * T:(q + 1) * T], start=True, stop=True)
                    ins.then_inc(hTd, 1)
                    pe.wait_ge(hTc, CR + g + 1)
                    pe.wait_ge(ysum, CR + g)
                    for q in range(G):
                        ins = pe.matmul(psA[:, q * T:(q + 1) * T], lhsT=hT[0:ADP + 1, q * T:(q + 1) * T], rhs=w12[p][0:ADP + 1, q, ADP:ADP + D], start=True, stop=True)
                    ins.then_inc(summed, 1)

                with pe.Fori(0, NG // NAB) as j:
                    for p in range(NAB):
                        adapter(j, p)

            @block.vector
            def _(dve):
                dve.sem_inc(ysum, CR)
                dve.sem_inc(stat, CR)
                dve.sem_inc(normed, CR)
                dve.wait_ge(a_ok, 1)
                dve.tensor_scalar(M["negA"][:, :, :], M["negA"][:, :, :], -1.0, None, ALU.mult)
                dve.wait_ge(moe_ld, 16 * 3)
                dve.tensor_scalar(K["wbc"][:, NE, :], K["sgp"][:, :], -1.0, 1.0, ALU.mult, ALU.add).then_inc(a_ok, 1)
                dve.wait_ge(a_ok, 2)
                dve.tensor_tensor(K["wbc"][:, 0:NE, :], K["wbc"][:, 0:NE, :], K["wbc"][:, NE, :].unsqueeze(1).broadcast_to([128, NE, NSEQ]), ALU.mult).then_inc(a_ok, 1)
                dve.wait_ge(a_ok, 3)
                dve.tensor_copy(K["wbc"][:, NE, :], K["sgp"][:, :])

                def adapter(j, p):
                    g = NAB * j + p
                    dve.wait_ge(summed, CR + g + 1)
                    dve.tensor_tensor(y[:, :, :], xg[p][:, :, :], psA[:, :].rearrange("p (q d) -> p q d", q=G), ALU.add).then_inc(ysum, 1)
                    dve.wait_ge(ysum, CR + g + 1)
                    for q in range(G):
                        ins = dve.bn_stats(stats[:, q, :], y[:, q, :])
                    ins.then_inc(normed, 1)
                    dve.wait_ge(normed, CR + 2 * g + 1)
                    dve.memset(spare[:, :], 0.0)
                    for q in range(G):
                        ins = dve.bn_aggr(mv[:, q, :], stats[:, q, :])
                    ins.then_inc(stat, 1)
                    dve.wait_ge(stat, CR + g + 1)
                    for q in range(G):
                        ins = dve.scalar_tensor_tensor(out=nrm[:, q, :], in0=y[:, q, :], scalar=mv[:, q, 0:1], in1=gb[p][:, q, 0, :], op0=ALU.subtract, op1=ALU.mult)
                    ins.then_inc(normed, 1)
                    dve.wait_ge(normed, CR + 2 * g + 2)
                    dve.wait_ge(rstd_ok, CR + g + 1)
                    for q in range(G):
                        ins = dve.scalar_tensor_tensor(out=K["h_res"][:, ds(g * G + q, 1), :].rearrange("p o d -> p (o d)"), in0=nrm[:, q, :], scalar=rstd[:, q:q + 1], in1=gb[p][:, q, 1, :], op0=ALU.mult, op1=ALU.add)
                    ins.then_inc(placed, 1)

                with dve.Fori(0, NG // NAB) as j:
                    for p in range(NAB):
                        adapter(j, p)


def mamba_phase(nc, A, K, M):
    ctx = ExitStack()
    with ctx:
        def sb(name, shape, dt=f32):
            return ctx.enter_context(nc.sbuf_tensor(name, shape, dt))

        def sem(name):
            return ctx.enter_context(nc.semaphore(name))

        taps, wz, wx, wdt, wo, par, negA, sel, xnT = (M[n] for n in ("taps", "wz", "wx", "wdt", "wo", "par", "negA", "sel", "xnT"))
        h_res, ident = K["h_res"], K["ident"]
        wcur = sb("wcur", [128, NTAP + 1, DI])
        wxcur = sb("wxcur", [128, NH, NX])
        wdcur = sb("wdcur", [64, DI])
        parc = sb("parc", [128, 8])
        Acur = [sb(f"Acur{p}", [128, NH * NS]) for p in range(2)]
        stats = sb("stats", [128, G, 6])
        mv = sb("mv", [128, G, 2])
        vare = sb("vare", [128, G])
        rstd = sb("rstd", [128, G])
        spare = sb("spare", [128, 1])
        xc = sb("xc", [128, G, D])
        u = sb("u", [128, NH, TOK])
        sz = [sb(f"sz{p}", [128, NH, TOK]) for p in range(2)]
        dt = [sb(f"dt{p}", [128, NH, G, T]) for p in range(2)]
        dtu = [sb(f"dtu{p}", [128, NH, TOK]) for p in range(2)]
        diag = sb("diag", [128, NH, 128])
        bc3 = [sb(f"bc3{p}", [96, TOK], bf16) for p in range(2)]
        xd = sb("xd", [64, TOK])
        mid = sb("mid", [32, TOK], bf16)
        r1 = sb("r1", [32, TOK])
        yg = sb("yg", [128, NH, TOK])
        crs = [sb(f"crs{b}", [128, TOK]) for b in range(NCS)]
        dA = [sb(f"dA{b}", [128, NH, G, T]) for b in range(NDA)]
        dB = [sb(f"dB{b}", [128, NH, TOK]) for b in range(NDB)]
        hh = [sb(f"hh{b}", [128, NH, TOK]) for b in range(NHB)]
        gg = [sb(f"gg{b}", [128, NH, TOK]) for b in range(NGB)]
        bank = [ctx.enter_context(nc.psum_tensor(f"bank{b}", [128, 512], f32)) for b in range(8)]
        psB, psC, psW = bank[0:2], bank[2], bank[3]
        psY = [bank[4:6], bank[6:8]]

        (wcur_ld, wready, wfree, brep, crep, dbu, da, scan, ccp, prod, paired, red, stat, moments, var_ok, rstd_ok, centred, skipped,
         par_ok, hi_ok, mid_ok, mids_ok, r1_ok, lo_ok, exp_ok, abs_ok, ln_ok, dt_ok, dtu_ok, diag_ok, silu_ok, ygated, zeroed) = (
            sem("m_" + n) for n in ("wcur_ld wready wfree brep crep dbu da scan ccp prod paired red stat moments var_ok rstd_ok centred skipped "
                                    "par_ok hi_ok mid_ok mids_ok r1_ok lo_ok exp_ok abs_ok ln_ok dt_ok dtu_ok diag_ok silu_ok ygated zeroed").split())

        def loop(eng, body, first, last):
            first()
            body(0, 0, False, True)
            with eng.Fori(0, (NIT - 2) // 2) as j:
                body(2 * j + 1, 1, True, True)
                body(2 * j + 2, 0, True, True)
            body(NIT - 1, 1, True, False)
            last()

        def use(b, c):
            if isinstance(b, int) and b == NIT - 1:
                c -= OUTP
            if isinstance(b, int) and b <= 0:
                return CR + 1 + (WUSE - 1) * (b + 1) + c - (c > OUTP)
            return CR + WUSE * b + WUSE - 1 + c

        def at_least(eng, sm, v):
            if not (isinstance(v, int) and v <= CR):
                eng.wait_ge(sm, v)

        with nc.Block() as block:
            @block.sync
            def _(sp):
                def weights(i):
                    lay = ds(i // NG, 1)
                    sp.dma_start(wcur[:, 0:NTAP, :], taps[:, lay, :, :].rearrange("p o k d -> p (o k) d")).then_inc(wcur_ld, 16)
                    sp.dma_start(wcur[:, NTAP:NTAP + 1, :], wz[:, lay, :]).then_inc(wcur_ld, 16)
                    sp.dma_start(wxcur[:, :, :], wx[:, ds(i // NG * NH, NH), :]).then_inc(wcur_ld, 16)
                    sp.dma_start(wdcur[32:32 + DTR, :], wdt[32:32 + DTR, lay, :].rearrange("p o d -> p (o d)")).then_inc(wcur_ld, 16)

                weights(0)
                for i in (1, 2):
                    sp.wait_ge(wready, use(i - 2, WUSE - 1))
                    weights(i)
                with sp.Fori(3, NIT) as i:
                    sp.wait_ge(wready, use(i - 2, WUSE - 1))
                    weights(i)

            @block.tensor
            def _(pe):
                for sm in (wready, brep, crep, red, skipped):
                    pe.sem_inc(sm, CR)

                def work(b, c):
                    at_least(pe, wfree, use(b, c))

                def broadcast_B(n, p, k):
                    at_least(pe, dbu, CR + n - 1)
                    pe.matmul(psB[k % 2][:, :], lhsT=sel[:, k, :], rhs=bc3[p][:, :], start=True, stop=True).then_inc(brep, 1)

                def broadcast_C(n, p, k):
                    at_least(pe, ccp, CR + n)
                    pe.matmul(psC[:, :], lhsT=sel[:, NS + k, :], rhs=bc3[p][:, :], start=True, stop=True).then_inc(crep, 1)

                def sum_states(n, p, k):
                    if k + 1 in PAIRED:
                        return
                    if k in PAIRED:
                        pe.wait_ge(paired, CR + (n - k) // NS * len(PAIRED) + PAIRED.index(k) + 1)
                    else:
                        pe.wait_ge(prod, CR + n + 1)
                    for c in range(NH):
                        ins = pe.matmul(psY[p][c][:, :], lhsT=ident[:, :], rhs=gg[k % NGB][:, c, :], start=False, stop=(k == NS - 1))
                    ins.then_inc(red, 2 if k in PAIRED else 1)

                def skip(t, p):
                    pe.wait_ge(diag_ok, CR + t + 1)
                    at_least(pe, ygated, CR + t - 1)
                    for c in range(NH):
                        ins = pe.matmul(psY[p][c][:, :], lhsT=diag[:, c, :], rhs=u[:, c, :], start=True, stop=False)
                    ins.then_inc(skipped, 1)

                def out_projection(b):
                    pe.wait_ge(ygated, CR + b)
                    if isinstance(b, int):
                        pe.wait_ge(wfree, use(b, OUTP) - 1)
                    else:
                        work(b, OUTP)
                    for q in range(G):
                        for c in range(NH):
                            ins = pe.matmul(psW[:, q * T:(q + 1) * T], lhsT=yg[:, c, q * T:(q + 1) * T],
                                            rhs=wo[:, ds((b - 1) // NG * NH + c, 1), :].rearrange("p o m -> p (o m)"), start=(c == 0), stop=(c == NH - 1))
                    ins.then_inc(wready, 1)

                def transposes(t):
                    pe.wait_ge(centred, CR + t + 1)
                    work(t - 2, 8)
                    for q in range(G):
                        ins = pe.transpose(psW[:, q * T:(q + 1) * T], xc[:, q, :], ident[:, :])
                    ins.then_inc(wready, 1)

                def pre(t, what):
                    b, c = t - 1, int(what[-1] == "1")
                    if what in ("x0", "more_x0", "x1", "more_x1"):
                        if what == "x0":
                            pe.wait_ge(wcur_ld, 64 * (t + 1))
                        if what[0] == "x":
                            work(b, c)
                        half = 0 if what[0] == "x" else NTAP // 2
                        for k in range(half, half + NTAP // 2):
                            ins = pe.matmul(psW[:, :], lhsT=wcur[:, k, c * 128:(c + 1) * 128], rhs=xnT[:, :, k:k + T], start=(k == 0), stop=(k == NTAP - 1))
                        if what[0] == "m":
                            ins.then_inc(wready, 1)
                    if what in ("z0", "z1"):
                        work(b, 2 + c)
                        pe.matmul(psW[:, :], lhsT=wcur[:, NTAP, c * 128:(c + 1) * 128], rhs=xnT[:, :, NTAP - 1:NTAP - 1 + T], start=True, stop=True).then_inc(wready, 1)
                    if what == "bcdt":
                        work(b, 5)
                        pe.wait_ge(silu_ok, CR + t + 1)
                        for c in range(NH):
                            ins = pe.matmul(psW[0:NX, :], lhsT=wxcur[:, c, :], rhs=u[:, c, :], start=(c == 0), stop=(c == NH - 1))
                        ins.then_inc(wready, 1)
                    if what in ("dt0", "dt1"):
                        work(b, 6 + c)
                        pe.matmul(psW[:, :], lhsT=wdcur[32:32 + DTR, c * 128:(c + 1) * 128], rhs=xd[32:32 + DTR, :], start=True, stop=True).then_inc(wready, 1)

                def parts(t):
                    pe.wait_ge(lo_ok, CR + t + 1)
                    pe.wait_ge(mids_ok, CR + t + 1)

                def first():
                    transposes(0)
                    for k in sorted(PE_AT):
                        for what in PE_AT[k]:
                            pre(0, what)
                    transposes(1)
                    skip(0, 0)
                    parts(0)
                    broadcast_B(0, 0, 0)
                    for k in range(CLEAD):
                        broadcast_C(k, 0, k)

                def body(i, p, prev, more):
                    for k in range(NS):
                        n = NS * i + k
                        if k < NS - 1:
                            broadcast_B(n + 1, p, k + 1)
                        elif more:
                            broadcast_B(n + 1, 1 - p, 0)
                        if k >= RLAG:
                            sum_states(n - RLAG, p, k - RLAG)
                        elif prev:
                            sum_states(n - RLAG, 1 - p, NS + k - RLAG)
                        if more:
                            for what in PE_AT.get(k, ()):
                                pre(i + 1, what)
                        if prev and k == OUT_AT:
                            out_projection(i)
                        if more and k == SKIP_AT:
                            skip(i + 1, 1 - p)
                        if more and k == TR_AT:
                            transposes(i + 2)
                        if k + CLEAD < NS:
                            broadcast_C(n + CLEAD, p, k + CLEAD)
                        elif more:
                            if k + CLEAD == NS:
                                parts(i + 1)
                            broadcast_C(n + CLEAD, 1 - p, k + CLEAD - NS)

                def last():
                    for k in range(NS - RLAG, NS):
                        sum_states(NS * (NIT - 1) + k, 1, k)
                    pe.wait_ge(ygated, CR + NIT)
                    pe.wait_ge(wfree, use(NIT - 1, OUTP + 1) - 1)
                    for q in range(G):
                        for c in range(NH):
                            ins = pe.matmul(psW[:, q * T:(q + 1) * T], lhsT=yg[:, c, q * T:(q + 1) * T], rhs=wo[:, (NL - 1) * NH + c, :], start=(c == 0), stop=(c == NH - 1))
                    ins.then_inc(wready, 1)

                loop(pe, body, first, last)

            @block.scalar
            def _(act):
                for sm in (par_ok, hi_ok, mids_ok, exp_ok, ln_ok, da, ccp, wfree, silu_ok):
                    act.sem_inc(sm, CR)

                def pre(t, what, p):
                    b, c = t - 1, int(what[-1] == "1")
                    if what == "params":
                        lay = ds(t // NG, 1)
                        at_least(act, diag_ok, CR + t)
                        act.activation(parc[:, :], par[:, lay, :].rearrange("p o v -> p (o v)"), ACT.Copy)
                        act.activation(Acur[p][:, :], negA[:, lay, :].rearrange("p o v -> p (o v)"), ACT.Copy).then_inc(par_ok, 1)
                        act.wait_ge(par_ok, CR + t + 1)
                    if what == "norm":
                        act.wait_ge(wready, use(t - 2, 8) + 1)
                        act.activation(xnT[:, :, NTAP - 1:NTAP - 1 + T], psW[:, :].rearrange("p (q t) -> p q t", q=G), ACT.Identity,
                                       scale=parc[:, 0:1], bias=parc[:, 1:2]).then_inc(wfree, 1)
                    if what in ("x0", "x1"):
                        act.wait_ge(wready, use(b, c) + 1)
                        if c == 0:
                            at_least(act, skipped, CR + t)
                            at_least(act, dtu_ok, CR + t)
                        act.activation(u[:, c, :], psW[:, :], ACT.Identity, bias=parc[:, 2 + c:3 + c]).then_inc(wfree, 1)
                    if what in ("z0", "z1"):
                        act.wait_ge(wready, use(b, 2 + c) + 1)
                        at_least(act, ygated, CR + t - 1)
                        act.activation(sz[p][:, c, :], psW[:, :], ACT.Copy).then_inc(wfree, 1)
                    if what == "silu":
                        act.wait_ge(wfree, use(b, 4))
                        act.activation(u[:, :, :], u[:, :, :], ACT.Silu).then_inc(silu_ok, 1)
                        act.activation(sz[p][:, :, :], sz[p][:, :, :], ACT.Silu)
                        act.preload_act_table_set(LNEXP)
                    if what == "bcdt":
                        act.wait_ge(wready, use(b, 5) + 1)
                        at_least(act, r1_ok, CR + t)
                        act.activation(xd[0:NX, :], psW[0:NX, :], ACT.Copy).then_inc(wfree, 1)
                        act.wait_ge(wfree, use(b, 6))
                        act.activation(bc3[p][0:32, :], xd[0:32, :], ACT.Copy).then_inc(hi_ok, 1)
                    if what in ("dt0", "dt1"):
                        act.wait_ge(wready, use(b, 6 + c) + 1)
                        at_least(act, dbu, CR + NS * (t - 1))
                        act.activation(dtu[p][:, c, :], psW[:, :], ACT.Identity, bias=parc[:, 4 + c:5 + c]).then_inc(wfree, 1)
                    if what == "mid":
                        act.wait_ge(mid_ok, CR + t + 1)
                        act.activation(bc3[p][32:64, :], mid[:, :], ACT.Copy).then_inc(mids_ok, 1)
                    if what == "softplus":
                        flat = dt[p][:, :, :, :].rearrange("p c q t -> p (c q t)")
                        act.wait_ge(abs_ok, CR + t + 1)
                        act.activation(flat, flat, ACT.Exp).then_inc(exp_ok, 1)
                        act.wait_ge(exp_ok, CR + t + 1)
                        act.activation(flat, flat, ACT.Ln, bias=1.0).then_inc(ln_ok, 1)

                def copy_C(i, k):
                    n = NS * i + k
                    act.wait_ge(crep, CR + n + 1)
                    at_least(act, prod, CR + n + 1 - NCS)
                    act.activation(crs[k % NCS][:, :], psC[:, :], ACT.Copy).then_inc(ccp, 1)

                def decay(i, p, k):
                    n = NS * i + k
                    if k == 0:
                        act.wait_ge(dt_ok, CR + i + 1)
                    at_least(act, scan, CR + n + 1 - NDA)
                    for c in range(NH):
                        ins = act.activation(dA[k % NDA][:, c, :, 1:T], dt[p][:, c, :, 1:T], ACT.Exp, scale=Acur[p][:, c * NS + k:c * NS + k + 1])
                    ins.then_inc(da, 1)

                def first():
                    for k in range(NS):
                        for what in ACT_AT.get(k, ()):
                            pre(0, what, 0)

                def body(i, p, prev, more):
                    for k in range(NS):
                        copy_C(i, k)
                        if more:
                            for what in ACT_AT.get(k, ()):
                                pre(i + 1, what, 1 - p)
                        decay(i, p, k)

                loop(act, body, first, lambda: None)

            @block.vector
            def _(dve):
                for sm in (lo_ok, mid_ok, dbu, scan, stat, moments, centred, abs_ok, dt_ok, dtu_ok, ygated, diag_ok):
                    dve.sem_inc(sm, CR)
                for b in range(NDA):
                    ins = dve.memset(dA[b][:, :, :, 0:1], 0.0)
                ins.then_inc(zeroed, 1)
                dve.wait_ge(zeroed, 1)

                def input_term(n, p, k):
                    dve.wait_ge(brep, CR + n + 1)
                    at_least(dve, scan, CR + n + 1 - NDB)
                    dve.tensor_tensor(dB[k % NDB][:, :, :], dtu[p][:, :, :], psB[k % 2][:, :].unsqueeze(1).broadcast_to([128, NH, TOK]), ALU.mult).then_inc(dbu, 1)

                def scan_step(n, p, k):
                    dve.wait_ge(da, CR + n + 1)
                    dve.wait_ge(dbu, CR + n + 1)
                    at_least(dve, prod, CR + n + 1 - NHB)
                    dve.tensor_tensor_scan(out=hh[k % NHB][:, :, :].rearrange("p c t -> p (c t)"), data0=dA[k % NDA][:, :, :, :].rearrange("p c q t -> p (c q t)"),
                                           data1=dB[k % NDB][:, :, :].rearrange("p c t -> p (c t)"), initial=0.0, op0=ALU.mult, op1=ALU.add).then_inc(scan, 1)

                def pre(t, what, p):
                    g = t % NG
                    if what == "moments":
                        at_least(dve, wfree, use(t - 2, 0))
                        for q in range(G):
                            ins = dve.bn_stats(stats[:, q, :], h_res[:, ds(g * G + q, 1), :].rearrange("p o d -> p (o d)"))
                        ins.then_inc(stat, 1)
                        dve.wait_ge(stat, CR + t + 1)
                        at_least(dve, centred, CR + t)
                        dve.memset(spare[:, :], 0.0)
                        for q in range(G):
                            ins = dve.bn_aggr(mv[:, q, :], stats[:, q, :])
                        ins.then_inc(moments, 1)
                    if what == "centre":
                        dve.wait_ge(rstd_ok, CR + t + 1)
                        at_least(dve, wready, use(t - 3, 8) + 1)
                        for q in range(G):
                            ins = dve.tensor_scalar(xc[:, q, :], h_res[:, ds(g * G + q, 1), :].rearrange("p o d -> p (o d)"), mv[:, q, 0:1], rstd[:, q:q + 1], ALU.subtract, ALU.mult)
                        ins.then_inc(centred, 1)
                    if what == "diag":
                        dve.wait_ge(silu_ok, CR + t + 1)
                        at_least(dve, skipped, CR + t)
                        for c in range(NH):
                            ins = dve.tensor_scalar(diag[:, c, :], ident[:, :], parc[:, 6 + c:7 + c], None, ALU.mult)
                        ins.then_inc(diag_ok, 1)
                    if what == "lo":
                        dve.wait_ge(r1_ok, CR + t + 1)
                        at_least(dve, mids_ok, CR + t)
                        dve.tensor_copy(mid[:, :], r1[:, :]).then_inc(mid_ok, 1)
                        dve.wait_ge(mid_ok, CR + t + 1)
                        dve.tensor_tensor(bc3[p][64:96, :], r1[:, :], mid[:, :], ALU.subtract).then_inc(lo_ok, 1)
                    vflat = dtu[p][:, :, :].rearrange("p c t -> p (c t)")
                    dflat = dt[p][:, :, :, :].rearrange("p c q t -> p (c q t)")
                    if what == "abs":
                        dve.wait_ge(wfree, use(t - 1, 8))
                        at_least(dve, da, CR + NS * (t - 1))
                        dve.scalar_tensor_tensor(out=dflat, in0=vflat, scalar=-1.0, in1=vflat, op0=ALU.mult, op1=ALU.min).then_inc(abs_ok, 1)
                    if what == "dt":
                        dve.wait_ge(ln_ok, CR + t + 1)
                        dve.scalar_tensor_tensor(out=dflat, in0=vflat, scalar=0.0, in1=dflat, op0=ALU.max, op1=ALU.add).then_inc(dt_ok, 1)
                        dve.wait_ge(dt_ok, CR + t + 1)
                        dve.tensor_tensor(vflat, dflat, u[:, :, :].rearrange("p c t -> p (c t)"), ALU.mult).then_inc(dtu_ok, 1)

                def gate(i, p):
                    dve.wait_ge(red, CR + NS * (i + 1))
                    dve.wait_ge(wready, use(i, OUTP) + 1)
                    for c in range(NH):
                        ins = dve.tensor_tensor(yg[:, c, :], sz[p][:, c, :], psY[p][c][:, :], ALU.mult)
                    ins.then_inc(ygated, 1)

                def residual(b):
                    dve.wait_ge(wready, use(b, OUTP) + 1)
                    at = ds((b - 1) % NG * G, G)
                    dve.tensor_tensor(h_res[:, at, :], h_res[:, at, :], psW[:, :].rearrange("p (q d) -> p q d", q=G), ALU.add).then_inc(wfree, 1)

                def first():
                    for t in range(2):
                        for what in ("moments", "centre"):
                            pre(t, what, t)
                    for what in ("diag", "lo", "abs", "dt"):
                        pre(0, what, 0)
                    dve.wait_ge(dtu_ok, CR + 1)
                    input_term(0, 0, 0)

                def body(i, p, prev, more):
                    for k in range(NS):
                        n = NS * i + k
                        for what in DVE_AT.get(k, ()):
                            if what == "gate" and prev:
                                gate(i - 1, 1 - p)
                            if what == "residual" and prev:
                                residual(i)
                            if more and what in ("moments", "centre"):
                                pre(i + 2, what, p)
                            if more and what in ("abs", "lo", "diag", "dt"):
                                pre(i + 1, what, 1 - p)
                        if k < NS - 1:
                            input_term(n + 1, p, k + 1)
                            scan_step(n, p, k)
                        elif more:
                            scan_step(n, p, k)
                            dve.wait_ge(dtu_ok, CR + i + 2)
                            input_term(n + 1, 1 - p, 0)
                        else:
                            scan_step(n, p, k)

                def last():
                    gate(NIT - 1, 1)
                    dve.wait_ge(wready, use(NIT - 1, OUTP + 1) + 1)
                    at = slice((NG - 1) * G, NG * G)
                    dve.tensor_tensor(h_res[:, at, :], h_res[:, at, :], psW[:, :].rearrange("p (q d) -> p q d", q=G), ALU.add)

                loop(dve, body, first, last)

            @block.gpsimd
            def _(pool):
                for sm in (prod, paired, rstd_ok, r1_ok):
                    pool.sem_inc(sm, CR)

                def pre(t, what, p):
                    if what == "rstd":
                        pool.wait_ge(moments, CR + t + 1)
                        pool.tensor_tensor(vare[:, :], mv[:, :, 1], K["eps"][:, :], ALU.add).then_inc(var_ok, 1)
                        pool.wait_ge(var_ok, t + 1)
                        at_least(pool, centred, CR + t)
                        pool.tensor_tensor(rstd[:, :], vare[:, :], K["nhalf"][:, :], ALU.pow).then_inc(rstd_ok, 1)
                    if what == "r1":
                        at_least(pool, lo_ok, CR + t)
                        pool.wait_ge(hi_ok, CR + t + 1)
                        pool.tensor_tensor(r1[:, :], xd[0:32, :], bc3[p][0:32, :], ALU.subtract).then_inc(r1_ok, 1)

                def first():
                    pre(0, "rstd", 0)
                    pre(1, "rstd", 1)
                    pre(0, "r1", 0)

                def body(i, p, prev, more):
                    for k in range(NS):
                        n = NS * i + k
                        if more and k == RSTD_AT:
                            pre(i + 2, "rstd", p)
                        if more and k == R1_AT:
                            pre(i + 1, "r1", 1 - p)
                        pool.wait_ge(scan, CR + n + 1)
                        pool.wait_ge(ccp, CR + n + 1)
                        at_least(pool, red, CR + n + 1 - NGB)
                        pool.tensor_tensor(gg[k % NGB][:, :, :], hh[k % NHB][:, :, :], crs[k % NCS][:, :].unsqueeze(1).broadcast_to([128, NH, TOK]), ALU.mult).then_inc(prod, 1)
                        if k in PAIRED:
                            pool.wait_ge(prod, CR + n + 1)
                            pool.tensor_tensor(gg[k % NGB][:, :, :], gg[k % NGB][:, :, :], gg[(k - 1) % NGB][:, :, :], ALU.add).then_inc(paired, 1)

                loop(pool, body, first, lambda: None)


def dense_phase(nc, A, K, x1_sb):
    ctx = ExitStack()
    with ctx:
        def sb(name, shape, dt=f32):
            return ctx.enter_context(nc.sbuf_tensor(name, shape, dt))

        def sem(name):
            return ctx.enter_context(nc.semaphore("d_" + name))

        NST = NE1 * NF
        NXW, NSG, NAC = 3, 3, 3
        DLAG = 2
        wgu, wbc, h_res, ident = K["wgu"], K["wbc"], K["h_res"], K["ident"]
        wdn = sb("wdn", [128, NE1, NF, D])
        xin = [sb(f"xin{p}", [128, G, D]) for p in range(2)]
        x1g = sb("x1g", [128, G, D])
        x1T = [sb(f"x1T{p}", [128, G, T]) for p in range(2)]
        xw = [sb(f"xw{b}", [128, G, T]) for b in range(NXW)]
        sg = [sb(f"sg{b}", [128, TOK]) for b in range(NSG)]
        ac = [sb(f"ac{b}", [128, TOK]) for b in range(NAC)]
        cT = sb("cT", [128, TOK])
        zrow = sb("zrow", [128, NSLOT * D // 128 // 8])
        bank = [ctx.enter_context(nc.psum_tensor(f"d_bank{b}", [128, 512], f32)) for b in range(8)]
        psG, psU, psD, psT, psM = bank[0:2], bank[2:4], bank[4], bank[5], bank[6:8]
        names = "x_ld0 x_ld1 zero zeroed x1 trans xT scaled gated upped silued acted summed sum_ok logits tokens log_ok tok_ok".split()
        Q = {n: sem(n) for n in names}
        w_ld = [sem(f"w_ld{e}") for e in range(NE1)]
        zero, zeroed, x1_ok, trans, xT_ok, scaled, gated, upped, silued, acted, summed, sum_ok, logits, tokens, log_ok, tok_ok = (
            Q[n] for n in ("zero zeroed x1 trans xT scaled gated upped silued acted summed sum_ok logits tokens log_ok tok_ok").split())
        x_ld = [Q["x_ld0"], Q["x_ld1"]]

        def at_least(eng, sm, v):
            if not (isinstance(v, int) and v <= CR):
                eng.wait_ge(sm, v)

        def loop(eng, first, body, last):
            first()
            body(0, 0, False, True)
            with eng.Fori(0, NG // 2 - 1) as j:
                body(2 * j + 1, 1, True, True)
                body(2 * j + 2, 0, True, True)
            body(NG - 1, 1, True, False)
            last(NG - 1)

        with nc.Block() as block:
            @block.sync
            def _(sp):
                def load_x(j, p):
                    at_least(sp, x1_ok, CR + 2 * j + p - 1)
                    sp.dma_start(xin[p][:, :, :], A["x"][ds((2 * j + p) * G, G), :, :].rearrange("b t d -> t b d")).then_inc(x_ld[p], 16)

                load_x(0, 0)
                load_x(0, 1)
                for e in range(NE):
                    sp.dma_start(wdn[:, e, :, :], A["Wd"][e].rearrange("(t p) d -> p t d", p=128)).then_inc(w_ld[e], 16)
                sp.dma_start(wdn[:, NE, :, :], A["Sd"].rearrange("(t p) d -> p t d", p=128)).then_inc(w_ld[NE], 16)
                with sp.Fori(1, NG // 2) as j:
                    load_x(j, 0)
                    load_x(j, 1)
                sp.wait_ge(zero, 1)
                for c in range(8):
                    sp.dma_start(A["disp"].rearrange("(c p n) d -> c p (n d)", c=8, p=128)[c], zrow[:, :]).then_inc(zeroed, 16)
                sp.wait_ge(zeroed, 16 * 8)

            @block.gpsimd
            def _(pool):
                pool.sem_inc(scaled, CR)
                pool.memset(zrow[:, :], 0.0).then_inc(zero, 1)

                def body(g, p):
                    for e in range(NE1):
                        m = NE1 * g + e
                        if e == 0:
                            pool.wait_ge(xT_ok, CR + g + 1)
                        at_least(pool, upped, CR + NF * (m - NXW) + NF)
                        pool.tensor_tensor(xw[(NE1 * p + e) % NXW][:, :, :], x1T[p][:, :, :],
                                           wbc[:, e, ds(G * g, G)].unsqueeze(2).broadcast_to([128, G, T]), ALU.mult).then_inc(scaled, 1)

                body(0, 0)
                body(1, 1)
                with pool.Fori(1, NG // 2) as j:
                    body(2 * j, 0)
                    body(2 * j + 1, 1)

            @block.tensor
            def _(pe):
                for sm in (trans, gated, upped, summed, logits, tokens):
                    pe.sem_inc(sm, CR)

                def transpose_x(g):
                    pe.wait_ge(x1_ok, CR + g + 1)
                    at_least(pe, xT_ok, CR + g)
                    for q in range(G):
                        ins = pe.transpose(psT[:, q * T:(q + 1) * T], x1g[:, q, :], ident[:, :])
                    ins.then_inc(trans, 1)

                def down(g, p, r):
                    n = NST * g + r
                    if r == 0:
                        at_least(pe, sum_ok, CR + g)
                    if isinstance(g, int) and g == 0 and r % NF == 0:
                        pe.wait_ge(w_ld[r // NF], 16)
                    pe.wait_ge(acted, CR + n + 1)
                    ins = pe.matmul(psD[:, :], lhsT=wdn[:, r // NF, r % NF, :], rhs=ac[r % NAC][:, :], start=(r == 0), stop=(r == NST - 1))
                    ins.then_inc(summed, 1)

                def post(g):
                    pe.wait_ge(sum_ok, CR + g + 1)
                    at_least(pe, log_ok, CR + g)
                    for q in range(G):
                        ins = pe.matmul(psM[0][:, q * NE:(q + 1) * NE], lhsT=cT[:, q * T:(q + 1) * T], rhs=K["wr"][:, :], start=True, stop=True)
                    ins.then_inc(logits, 1)
                    at_least(pe, tok_ok, CR + g)
                    for q in range(G):
                        ins = pe.transpose(psM[1][:, q * T:(q + 1) * T], cT[:, q * T:(q + 1) * T], ident[:, :])
                    ins.then_inc(tokens, 1)

                def body(g, p, prev, more):
                    for r in range(NST):
                        n = NST * g + r
                        e, f = r // NF, r % NF
                        if r == 0:
                            pe.wait_ge(xT_ok, CR + g + 1)
                        at_least(pe, silued, CR + n - 1)
                        pe.matmul(psG[r % 2][:, :], lhsT=wgu[:, e, 0, f * 128:(f + 1) * 128], rhs=x1T[p][:, :, :], start=True, stop=True).then_inc(gated, 1)
                        if f == 0:
                            pe.wait_ge(scaled, CR + NE1 * g + e + 1)
                        at_least(pe, acted, CR + n - 1)
                        pe.matmul(psU[r % 2][:, :], lhsT=wgu[:, e, 1, f * 128:(f + 1) * 128], rhs=xw[(NE1 * p + e) % NXW][:, :, :], start=True, stop=True).then_inc(upped, 1)
                        if r >= DLAG:
                            down(g, p, r - DLAG)
                        if more and r == 12:
                            transpose_x(g + 1)
                        if prev and r == DLAG + 1:
                            post(g - 1)
                    for r in range(NST - DLAG, NST):
                        down(g, p, r)

                def first():
                    transpose_x(0)
                    pe.wait_ge(K["wgu_ld"], 16 * 4)

                loop(pe, first, body, post)

            @block.scalar
            def _(act):
                for sm in (xT_ok, silued, sum_ok, tok_ok):
                    act.sem_inc(sm, CR)

                def copy_x(g, p):
                    act.wait_ge(trans, CR + g + 1)
                    at_least(act, upped, CR + NST * (g - 1))
                    act.activation(x1T[p][:, :, :].rearrange("p q t -> p (q t)"), psT[:, :], ACT.Copy).then_inc(xT_ok, 1)

                def tokens_out(g):
                    act.wait_ge(tokens, CR + g + 1)
                    act.activation(h_res[:, ds(g * G, G), :].rearrange("p q d -> p (q d)"), psM[1][:, :], ACT.Copy).then_inc(tok_ok, 1)

                def body(g, p, prev, more):
                    for r in range(NST):
                        n = NST * g + r
                        if prev and r == 8:
                            tokens_out(g - 1)
                        act.wait_ge(gated, CR + n + 1)
                        at_least(act, acted, CR + n + 1 - NSG)
                        act.activation(sg[r % NSG][:, :], psG[r % 2][:, :], ACT.Silu).then_inc(silued, 1)
                        if more and r == 14:
                            copy_x(g + 1, 1 - p)
                    act.wait_ge(summed, CR + NST * (g + 1))
                    at_least(act, tokens, CR + g)
                    act.activation(cT[:, :], psD[:, :], ACT.Copy).then_inc(sum_ok, 1)

                loop(act, lambda: copy_x(0, 0), body, tokens_out)

            @block.vector
            def _(dve):
                for sm in (x1_ok, acted, log_ok):
                    dve.sem_inc(sm, CR)

                def residual(g, p):
                    at_least(dve, trans, CR + g)
                    dve.wait_ge(x_ld[p], 16 * (g // 2 + 1) if isinstance(g, int) else 8 * (g - p + 2))
                    dve.tensor_tensor(x1g[:, :, :], xin[p][:, :, :], h_res[:, ds(g * G, G), :], ALU.add)
                    dve.tensor_tensor(x1_sb[:, ds(g * G, G), :], xin[p][:, :, :], h_res[:, ds(g * G, G), :], ALU.add).then_inc(x1_ok, 1)

                def logits_out(g):
                    dve.wait_ge(logits, CR + g + 1)
                    dve.tensor_copy(K["lg"][:, ds(g * G, G), :].rearrange("p q e -> p (q e)"), psM[0][:, 0:G * NE]).then_inc(log_ok, 1)

                def body(g, p, prev, more):
                    for r in range(NST):
                        n = NST * g + r
                        if more and r == 4:
                            residual(g + 1, 1 - p)
                        if prev and r == 8:
                            logits_out(g - 1)
                        dve.wait_ge(silued, CR + n + 1)
                        dve.wait_ge(upped, CR + n + 1)
                        at_least(dve, summed, CR + n + 1 - NAC)
                        dve.tensor_tensor(ac[r % NAC][:, :], sg[r % NSG][:, :], psU[r % 2][:, :], ALU.mult).then_inc(acted, 1)

                loop(dve, lambda: residual(0, 0), body, logits_out)


def router_phase(nc, A, K):
    ctx = ExitStack()
    with ctx:
        def sb(name, shape, dt=f32):
            return ctx.enter_context(nc.sbuf_tensor(name, shape, dt))

        all_e = [128, NSEQ, NE]
        lg = K["lg"]
        gates, m1, m2, l2, tmp, score, pos, tot, cum = (sb("r_" + n, all_e) for n in "gates m1 m2 l2 tmp score pos tot cum".split())
        mx, den, g1, g2, s1, s2, b1, b2, keep = (sb("r_" + n, [128, NSEQ]) for n in "mx den g1 g2 s1 s2 b1 b2 keep".split())
        rank = sb("r_rank", [128, NE])
        base = sb("r_base", [128, NE])
        one_t = sb("r_one_t", [128, NSEQ])
        kept = [sb(f"r_kept{c}", [128, NSEQ]) for c in range(2)]
        tri = sb("tri", [128, 128])
        ones = sb("ones", [128, 128])
        psP = ctx.enter_context(nc.psum_tensor("r_psP", [128, 512], f32))
        psS = ctx.enter_context(nc.psum_tensor("r_psS", [128, 512], f32))
        made, chain, expd, masked, counted, slots, pch = (ctx.enter_context(nc.semaphore("r_" + n)) for n in "made chain expd masked counted slots pch".split())

        def over_e(v):
            return v[:, :].unsqueeze(2).broadcast_to(all_e)

        def over_t(v):
            return v[:, :].unsqueeze(1).broadcast_to(all_e)

        with nc.Block() as block:
            @block.gpsimd
            def _(pool):
                n = 0

                def link(ins):
                    nonlocal n
                    n += 1
                    ins.then_inc(pch, 1)
                    pool.wait_ge(pch, n)

                link(pool.memset(ones[:, :], 1.0))
                link(pool.memset(one_t[:, :], 1.0))
                link(pool.affine_select(out=tri[:, :], in_=ones[:, :], compare_op=ALU.is_gt, fill=0.0, base=0, pattern=[[1, 128]], channel_multiplier=-1))
                for e in range(NE):
                    pool.memset(rank[:, e:e + 1], float(NE - e))
                    ins = pool.memset(base[:, e:e + 1], float(e * CAP))
                ins.then_inc(made, 1)
                pool.wait_ge(slots, 1)
                for b in range(NSEQ):
                    pool.indirect_dma_start(A["disp"], bass.IndirectOffsetOnAxis(ap=K["scatter"][0][:, b:b + 1], axis=0),
                                            K["h_res"][:, b, :], None, bounds_check=NSLOT - 1, oob_is_err=False).then_inc(K["scattered"], 16)

            @block.scalar
            def _(act):
                act.wait_ge(masked, 1)
                act.activation(gates[:, :, :], tmp[:, :, :], ACT.Exp).then_inc(expd, 1)

            @block.tensor
            def _(pe):
                for c, m in ((0, m1), (1, m2)):
                    pe.wait_ge(masked, 2 + c)
                    if c == 0:
                        pe.wait_ge(made, 1)
                    else:
                        pe.wait_ge(counted, 2)
                    pe.matmul(psP[:, 0:NSEQ * NE], lhsT=tri[:, :], rhs=m[:, :, :].rearrange("p b e -> p (b e)"), start=True, stop=True)
                    pe.matmul(psS[:, 0:NSEQ * NE], lhsT=ones[:, :], rhs=m[:, :, :].rearrange("p b e -> p (b e)"), start=True, stop=True).then_inc(counted, 1)

            @block.vector
            def _(dve):
                n = 0

                def link(ins):
                    nonlocal n
                    n += 1
                    ins.then_inc(chain, 1)
                    dve.wait_ge(chain, n)

                def tt(o, a, b, op):
                    link(dve.tensor_tensor(o, a, b, op))

                def reduced(o, a, op):
                    link(dve.tensor_reduce(o, a, AX.X, op))

                def first_of(m, vals, best):
                    tt(tmp[:, :, :], vals, over_e(best), ALU.is_equal)
                    tt(score[:, :, :], tmp[:, :, :], over_t(rank), ALU.mult)
                    reduced(keep[:, :], score[:, :, :], ALU.max)
                    tt(m, score[:, :, :], over_e(keep), ALU.is_equal)

                def place(c, m):
                    dve.wait_ge(counted, 2 * c + 1)
                    link(dve.tensor_copy(tot[:, :, :].rearrange("p b e -> p (b e)"), psS[:, 0:NSEQ * NE]))
                    for e in range(NE):
                        start = 0.0 if c == 0 else s2[:, e:e + 1]
                        ins = dve.tensor_tensor_scan(out=cum[:, :, e], data0=one_t[:, :], data1=tot[:, :, e], initial=start, op0=ALU.mult, op1=ALU.add)
                    link(ins)
                    tt(pos[:, :, :], cum[:, :, :], tot[:, :, :], ALU.subtract)
                    if c == 0:
                        link(dve.tensor_copy(s2[:, 0:NE], cum[:, NSEQ - 1, :]))
                    dve.tensor_tensor(pos[:, :, :], pos[:, :, :], psP[:, 0:NSEQ * NE].rearrange("p (b e) -> p b e", e=NE), ALU.add).then_inc(counted, 1)
                    dve.wait_ge(counted, 2 * c + 2)
                    tt(tmp[:, :, :], pos[:, :, :], m[:, :, :], ALU.mult)
                    reduced(s1[:, :], tmp[:, :, :], ALU.add)
                    tt(tmp[:, :, :], m[:, :, :], over_t(base), ALU.mult)
                    reduced(b1[:, :], tmp[:, :, :], ALU.add)
                    link(dve.tensor_scalar(kept[c][:, :], s1[:, :], float(CAP), None, ALU.is_lt))
                    link(dve.scalar_tensor_tensor(out=b1[:, :], in0=s1[:, :], scalar=float(CAP - 1), in1=b1[:, :], op0=ALU.min, op1=ALU.add))
                    link(dve.tensor_scalar(b2[:, :], kept[c][:, :], -FAR, FAR, ALU.mult, ALU.add))
                    tt(b2[:, :], b1[:, :], b2[:, :], ALU.add)
                    dve.tensor_copy(K["scatter"][c][:, :], b2[:, :]).then_inc(slots, 1)
                    dve.wait_ge(slots, c + 1)
                    link(dve.tensor_copy(K["gather"][c][:, :], b1[:, :]))

                dve.wait_ge(made, 1)
                reduced(mx[:, :], lg[:, :, :], ALU.max)
                dve.tensor_tensor(tmp[:, :, :], lg[:, :, :], over_e(mx), ALU.subtract).then_inc(masked, 1)
                dve.wait_ge(expd, 1)
                reduced(den[:, :], gates[:, :, :], ALU.add)
                link(dve.reciprocal(den[:, :], den[:, :]))
                tt(gates[:, :, :], gates[:, :, :], over_e(den), ALU.mult)
                reduced(mx[:, :], gates[:, :, :], ALU.max)
                first_of(m1[:, :, :], gates[:, :, :], mx)
                link(dve.tensor_scalar(l2[:, :, :], m1[:, :, :], -3.0e38, None, ALU.mult))
                dve.tensor_tensor(l2[:, :, :], l2[:, :, :], lg[:, :, :], ALU.add).then_inc(masked, 1)
                dve.wait_ge(masked, 2)
                place(0, m1)
                reduced(mx[:, :], l2[:, :, :], ALU.max)
                first_of(m2[:, :, :], l2[:, :, :], mx)
                tt(tmp[:, :, :], gates[:, :, :], m1[:, :, :], ALU.mult)
                reduced(g1[:, :], tmp[:, :, :], ALU.add)
                dve.tensor_tensor(tmp[:, :, :], gates[:, :, :], m2[:, :, :], ALU.mult).then_inc(masked, 1)
                dve.wait_ge(masked, 3)
                reduced(g2[:, :], tmp[:, :, :], ALU.add)
                tt(den[:, :], g1[:, :], g2[:, :], ALU.add)
                link(dve.tensor_scalar(den[:, :], den[:, :], 1e-9, None, ALU.max))
                link(dve.reciprocal(den[:, :], den[:, :]))
                tt(g1[:, :], g1[:, :], den[:, :], ALU.mult)
                tt(g2[:, :], g2[:, :], den[:, :], ALU.mult)
                place(1, m2)
                for c, (g, w) in enumerate(((g1, K["w1"]), (g2, K["w2"]))):
                    link(dve.tensor_tensor(w[:, :], g[:, :], kept[c][:, :], ALU.mult))


def sparse_phase(nc, A, K, x1_sb, out):
    ctx = ExitStack()
    with ctx:
        def sb(name, shape, dt=f32):
            return ctx.enter_context(nc.sbuf_tensor(name, shape, dt))

        def sem(name):
            return ctx.enter_context(nc.semaphore("e_" + name))

        NO = 4
        NHT = CAP // 512
        wg = [sb(f"ewg{p}", [128, F]) for p in range(2)]
        wd = [sb(f"ewd{p}", [128, NF, D]) for p in range(2)]
        dx = [sb(f"dx{p}", [128, NCH, D]) for p in range(2)]
        dT = [sb(f"dT{b}", [128, 512]) for b in range(2)]
        ht = [sb(f"ht{b}", [128, NF, 512]) for b in range(2)]
        eos = [sb(f"eos{p}", [128, NCH, D]) for p in range(2)]
        got = [[sb(f"got{c}_{b}", [128, D]) for b in range(NO)] for c in range(2)]
        part = [sb(f"part{b}", [128, D]) for b in range(NO)]
        fin = [sb(f"fin{b}", [128, D]) for b in range(NO)]
        bank = [ctx.enter_context(nc.psum_tensor(f"e_bank{b}", [128, 512], f32)) for b in range(8)]
        psT, psH, psE = bank[0:2], bank[2:6], bank[6:8]
        w_ld, x_ld = [sem("w_ld0"), sem("w_ld1")], [sem("x_ld0"), sem("x_ld1")]
        trans, copied, upped, gelud, downed, evac, stored = (sem(n) for n in "trans copied upped gelud downed evac stored".split())
        gat = [sem(f"gat{b}") for b in range(NO)]
        outs = [sem(f"outs{b}") for b in range(NO)]
        partd, find = sem("partd"), sem("find")
        disp, eo = A["disp"], A["eo"]

        def at_least(eng, sm, v):
            if not (isinstance(v, int) and v <= CR):
                eng.wait_ge(sm, v)

        def experts(eng, body):
            with eng.Fori(0, NE // 2) as j:
                body(2 * j, 0, j)
                body(2 * j + 1, 1, j)

        with nc.Block() as block:
            @block.sync
            def _(sp):
                sp.sem_inc(stored, 16)

                def load(e, p):
                    at_least(sp, evac, CR + NHT * (e - 1))
                    sp.dma_start(wg[p][:, :], A["w_gate"][ds(e, 1), :, :].rearrange("o d f -> (o d) f")).then_inc(w_ld[p], 16)
                    sp.dma_start(wd[p][:, :, :], A["w_down"][ds(e, 1), :, :].rearrange("o (t p) d -> p (o t) d", p=128)).then_inc(w_ld[p], 16)
                    if isinstance(e, int) and e == 0:
                        sp.wait_ge(K["scattered"], 16 * 2 * NSEQ)
                    sp.dma_start(dx[p][:, :, :], disp[ds(e * CAP, CAP), :].rearrange("(c p) d -> p c d", p=128)).then_inc(x_ld[p], 16)

                def store(e, p):
                    sp.wait_ge(evac, CR + NHT * (e + 1))
                    sp.dma_start(eo[ds(e * CAP, CAP), :].rearrange("(c p) d -> p c d", p=128), eos[p][:, :, :]).then_inc(stored, 16)

                load(0, 0)
                load(1, 1)
                with sp.Fori(0, NE // 2 - 1) as j:
                    store(2 * j, 0)
                    load(2 * j + 2, 0)
                    store(2 * j + 1, 1)
                    load(2 * j + 3, 1)
                store(NE - 2, 0)
                store(NE - 1, 1)
                for b in range(NSEQ):
                    sp.wait_ge(find, b + 1)
                    sp.dma_start(out[b], fin[b % NO][:, :]).then_inc(outs[b % NO], 16)
                for b in range(NO):
                    sp.wait_ge(outs[b], 16 * NSEQ // NO)

            @block.gpsimd
            def _(pool):
                for b in range(NSEQ):
                    pool.indirect_dma_start(disp, bass.IndirectOffsetOnAxis(ap=K["scatter"][1][:, b:b + 1], axis=0),
                                            K["h_res"][:, b, :], None, bounds_check=NSLOT - 1, oob_is_err=False).then_inc(K["scattered"], 16)
                pool.wait_ge(stored, 16 + 16 * NE)
                for b in range(NSEQ):
                    if b >= NO:
                        pool.wait_ge(find, b + 1 - NO)
                    for c in range(2):
                        pool.indirect_dma_start(got[c][b % NO][:, :], None, eo,
                                                bass.IndirectOffsetOnAxis(ap=K["gather"][c][:, b:b + 1], axis=0)).then_inc(gat[b % NO], 16)

            @block.tensor
            def _(pe):
                for sm in (trans, upped, downed):
                    pe.sem_inc(sm, CR)

                def up(e, p, j, c):
                    h = NHT * e + c
                    if c == 0:
                        pe.wait_ge(x_ld[p], 16 * (j + 1))
                        pe.wait_ge(w_ld[p], 32 * (j + 1))
                    at_least(pe, copied, CR + h - 1)
                    for q in range(4):
                        ins = pe.transpose(psT[c][:, q * 128:(q + 1) * 128], dx[p][:, 4 * c + q, :], K["ident"][:, :])
                    ins.then_inc(trans, 1)
                    pe.wait_ge(copied, CR + h + 1)
                    for f in range(NF):
                        at_least(pe, gelud, CR + NF * (h - 1) + f + 1)
                        pe.matmul(psH[f][:, :], lhsT=wg[p][:, f * 128:(f + 1) * 128], rhs=dT[c][:, :], start=True, stop=True).then_inc(upped, 1)

                def down(e, p, c):
                    h = NHT * e + c
                    pe.wait_ge(gelud, CR + NF * (h + 1))
                    at_least(pe, evac, CR + h - 1)
                    for q in range(4):
                        for f in range(NF):
                            ins = pe.matmul(psE[c][:, q * 128:(q + 1) * 128], lhsT=ht[c][:, f, q * 128:(q + 1) * 128], rhs=wd[p][:, f, :], start=(f == 0), stop=(f == NF - 1))
                    ins.then_inc(downed, 1)

                def body(e, p, j):
                    up(e, p, j, 0)
                    up(e, p, j, 1)
                    down(e, p, 0)
                    down(e, p, 1)

                experts(pe, body)

            @block.scalar
            def _(act):
                act.sem_inc(gelud, CR)

                def body(e, p, j):
                    for c in range(NHT):
                        h = NHT * e + c
                        at_least(act, downed, CR + h - 1)
                        for f in range(NF):
                            act.wait_ge(upped, CR + NF * h + f + 1)
                            act.activation(ht[c][:, f, :], psH[f][:, :], ACT.Gelu).then_inc(gelud, 1)

                experts(act, body)

            @block.vector
            def _(dve):
                dve.sem_inc(copied, CR)
                dve.sem_inc(evac, CR)

                def body(e, p, j):
                    for c in range(NHT):
                        h = NHT * e + c
                        dve.wait_ge(trans, CR + h + 1)
                        at_least(dve, upped, CR + NF * (h - 1))
                        dve.tensor_copy(dT[c][:, :], psT[c][:, :]).then_inc(copied, 1)
                    for c in range(NHT):
                        h = NHT * e + c
                        dve.wait_ge(downed, CR + h + 1)
                        dve.wait_ge(stored, 16 + 16 * (e - 1))
                        dve.tensor_copy(eos[p][:, 4 * c:4 * c + 4, :].rearrange("p q d -> p (q d)"), psE[c][:, :]).then_inc(evac, 1)

                experts(dve, body)
                for b in range(NSEQ):
                    dve.wait_ge(gat[b % NO], 32 * (b // NO + 1))
                    dve.scalar_tensor_tensor(out=part[b % NO][:, :], in0=got[0][b % NO][:, :], scalar=K["w1"][:, b:b + 1], in1=x1_sb[:, b, :], op0=ALU.mult, op1=ALU.add).then_inc(partd, 1)
                    dve.wait_ge(partd, b + 1)
                    if b >= NO:
                        dve.wait_ge(outs[b % NO], 16 * (b // NO))
                    dve.scalar_tensor_tensor(out=fin[b % NO][:, :], in0=got[1][b % NO][:, :], scalar=K["w2"][:, b:b + 1], in1=part[b % NO][:, :], op0=ALU.mult, op1=ALU.add).then_inc(find, 1)


def mega(nc, A, out):
    ctx = ExitStack()
    with ctx:
        def sb(c, name, shape, dt=f32):
            return c.enter_context(nc.sbuf_tensor(name, shape, dt))

        K = {
            "h_res": sb(ctx, "h_res", [128, NSEQ, D]),
            "ident": sb(ctx, "ident", [128, 128]),
            "eps": sb(ctx, "eps", [128, G]),
            "nhalf": sb(ctx, "nhalf", [128, G]),
            "wgu": sb(ctx, "wgu", [128, NE1, 2, F]),
            "scattered": ctx.enter_context(nc.semaphore("scattered")),
            "wgu_ld": ctx.enter_context(nc.semaphore("wgu_ld")),
            "wbc": sb(ctx, "wbc", [128, NE1, NSEQ]),
            "sgp": sb(ctx, "sgp", [128, NSEQ]),
            "wr": sb(ctx, "wr", [128, NE]),
        }
        with ExitStack() as c2:
            M = {
                "taps": sb(c2, "taps", [128, NL, NTAP, DI]),
                "wz": sb(c2, "wz", [128, NL, DI]),
                "wx": sb(c2, "wx", [128, NL * NH, NX]),
                "wdt": sb(c2, "wdt", [64, NL, DI]),
                "wo": sb(c2, "wo", [128, NL * NH, D]),
                "par": sb(c2, "par", [128, NL, 8]),
                "negA": sb(c2, "negA", [128, NL, NH * NS]),
                "sel": sb(c2, "sel", [96, 2 * NS, 128], bf16),
                "xnT": sb(c2, "xnT", [128, G, T + NTAP - 1]),
            }
            M["zpad"] = M["xnT"][:, :, 0:NTAP - 1]
            setup_phase(nc, A, K, M)
            mamba_phase(nc, A, K, M)
        with ExitStack() as c5:
            x1_sb = sb(c5, "x1_sb", [128, NSEQ, D])
            K["lg"] = sb(c5, "lg", [128, NSEQ, NE])
            K["w1"], K["w2"] = sb(c5, "gw1", [128, NSEQ]), sb(c5, "gw2", [128, NSEQ])
            K["scatter"] = [sb(c5, f"scatter{c}", [128, NSEQ], u32) for c in range(2)]
            K["gather"] = [sb(c5, f"gather{c}", [128, NSEQ], u32) for c in range(2)]
            dense_phase(nc, A, K, x1_sb)
            router_phase(nc, A, K)
            sparse_phase(nc, A, K, x1_sb, out)


def kernel(**inputs):
    import numpy as np
    import concourse.bacc as bacc
    from concourse.bass_utils import run_bass_kernel_spmd

    I = {k: np.asarray(v) for k, v in inputs.items()}
    c = np.ascontiguousarray

    def halves(a):
        return a.reshape(NL, NH, 128).transpose(2, 0, 1)

    perm = list(range(DTR, NX)) + list(range(DTR))
    par = np.concatenate([I["L0_attn_ln_w"].T[:, :, None], I["L0_attn_ln_b"].T[:, :, None], halves(I["L0_attn_conv_b"]),
                          halves(I["L0_attn_b_dt"]), halves(I["L0_attn_Dp"])], axis=2)
    W12 = np.zeros((NLANG, D, ADP + D + 1), I["L0_cond_W1"].dtype)
    W12[:, :, :ADP], W12[:, :ADP, ADP:ADP + D] = I["L0_cond_W1"], I["L0_cond_W2"]
    W12[:, ADP, ADP:ADP + D], W12[:, :ADP, ADP + D] = I["L0_cond_b2"], I["L0_cond_b1"]
    arrays = {
        "x": I["x"], "ids": I["itok_B_0_8"].reshape(1, NSEQ), "gateT": I["fside_Bx8_0"].T, "sgate": I["condB_sharedgateprob"].reshape(1, NSEQ),
        "W12": W12, "gb": np.stack([I["L0_cond_gamma"], I["L0_cond_beta"]], axis=1),
        "W_inT": I["L0_attn_W_in"].transpose(0, 2, 1), "conv_wT": I["L0_attn_conv_w"].transpose(0, 2, 1),
        "W_xT": I["L0_attn_W_x"][:, perm, :].transpose(0, 2, 1), "W_dtT": I["L0_attn_W_dt"].transpose(0, 2, 1),
        "W_outT": I["L0_attn_W_out"].transpose(0, 2, 1), "par": par,
        "A_log": I["L0_attn_A_log"].reshape(NL, NH, 128, NS).transpose(2, 0, 1, 3).reshape(128, NL, NH * NS),
        "Wg": I["L0_cond2_Wg"], "Wu": I["L0_cond2_Wu"], "Wd": I["L0_cond2_Wd"],
        "Sg": I["L0_cond2_Sg"], "Su": I["L0_cond2_Su"], "Sd": I["L0_cond2_Sd"],
        "wg": I["L0_ffn_wg"], "w_gate": I["L0_ffn_w_gate"], "w_down": I["L0_ffn_w_down"],
    }
    nc = bacc.Bacc("TRN2", target_bir_lowering=False, num_devices=1)
    arrays = {f"in_{k}": c(v) for k, v in arrays.items()}
    A = {k[3:]: nc.dram_tensor(k, v.shape, mybir.dt.from_np(v.dtype), kind="ExternalInput").ap() for k, v in arrays.items()}
    A["disp"] = nc.dram_tensor("disp", (NSLOT, D), f32, kind="Internal").ap()
    A["eo"] = nc.dram_tensor("eo", (NSLOT, D), f32, kind="Internal").ap()
    out = nc.dram_tensor("out", (NSEQ, T, D), f32, kind="ExternalOutput").ap()
    mega(nc, A, out)
    r = run_bass_kernel_spmd(nc, [arrays], core_ids=[0])
    return r.results[0]["out"]
```
